# Optimizing a Trainium2 kernel written in Bass

```python
import numpy as np
import jax
import jax.numpy as jnp

def _softmax(x, axis=-1):
    return jax.nn.softmax(x, axis=axis)

def _gelu(x):
    return jax.nn.gelu(x, approximate=True)

def _silu(x):
    return jax.nn.silu(x)

def _sigmoid(x):
    return jax.nn.sigmoid(x)

def _layernorm(x, axis=-1, eps=1e-05):
    m = jnp.mean(x, axis=axis, keepdims=True)
    v = jnp.var(x, axis=axis, keepdims=True)
    return (x - m) / jnp.sqrt(v + eps)

def _scatter_add(tgt, idx, src, axis=0):
    return tgt.at[idx].add(src)

def _segment_sum(src, seg, n):
    return jax.ops.segment_sum(src, seg, n)
kernel_name = 'mk_adj_preln_d2_adj_r2_d075bb'

def setup_inputs(seed: int=0):
    np.random.seed(seed)
    _w = jnp.asarray

    def _rec_inputs():
        import jax
        import jax.numpy as jnp
        _gk = jax.random.key(seed)
        x = -0.0005207 + 1.001 * jax.random.normal(jax.random.fold_in(_gk, 1), (8192, 128), jnp.float32)
        _a = jax.random.bernoulli(jax.random.fold_in(_gk, 2), 0.000244141, (8192, 8192))
        _a = jnp.logical_or(_a, jnp.swapaxes(_a, -1, -2))
        _a = jnp.logical_or(_a, jnp.eye(8192, dtype=bool))
        adj = _a.astype(jnp.int32)
        return (x, adj)
    x, adj = _rec_inputs()

    def _L0_gnn_setup():
        import jax, jax.numpy as jnp
        import numpy as np
        N = 4096
        D_IN = 128
        D_OUT = 128
        ALPHA = 0.2
        key = jax.random.key(seed)
        k_x, k_adj, k_w, k_a1, k_a2 = jax.random.split(key, 5)
        xx = jax.random.normal(k_x, (N, D_IN), dtype=jnp.float32)
        adj_hat = jax.random.randint(k_adj, (N, N), 0, 2, dtype=jnp.int32)
        weight = jax.random.normal(k_w, (D_IN, D_OUT), dtype=jnp.float32) * (1.0 / np.sqrt(D_IN))
        weight_a1 = jax.random.normal(k_a1, (D_OUT, 1), dtype=jnp.float32) * (1.0 / np.sqrt(D_OUT))
        weight_a2 = jax.random.normal(k_a2, (D_OUT, 1), dtype=jnp.float32) * (1.0 / np.sqrt(D_OUT))
        return {'xx': xx, 'adj_hat': adj_hat, 'weight': weight, 'weight_a1': weight_a1, 'weight_a2': weight_a2}
    _L0_gnn_all = _L0_gnn_setup()
    _L0_gnn_in = {k: v for k, v in _L0_gnn_all.items() if k in ('weight', 'weight_a1', 'weight_a2')}
    del _L0_gnn_all

    def _L1_gnn_setup():
        import jax, jax.numpy as jnp
        import numpy as np
        N = 3072
        IN_DIM = 128
        OUT_DIM = 128
        NUM_HEADS = 4
        HEAD_DIM = OUT_DIM // NUM_HEADS
        NEG_SLOPE = 0.2
        key = jax.random.key(seed)
        k_x, k_adj, k_W, k_a = jax.random.split(key, 4)
        x = jax.random.normal(k_x, (N, IN_DIM), dtype=jnp.float32)
        adj = jax.random.randint(k_adj, (N, N), 0, 2, dtype=jnp.int32)
        W = jax.random.normal(k_W, (IN_DIM, OUT_DIM), dtype=jnp.float32) / np.sqrt(IN_DIM)
        a = jax.random.normal(k_a, (2 * HEAD_DIM,), dtype=jnp.float32) / np.sqrt(2 * HEAD_DIM)
        return {'x': x, 'adj': adj, 'W': W, 'a': a}
    _L1_gnn_all = _L1_gnn_setup()
    _L1_gnn_in = {k: v for k, v in _L1_gnn_all.items() if k in ('W', 'a')}
    del _L1_gnn_all
    return {'x': x, 'adj': adj, 'L0_gnn_weight': _L0_gnn_in['weight'], 'L0_gnn_weight_a1': _L0_gnn_in['weight_a1'], 'L0_gnn_weight_a2': _L0_gnn_in['weight_a2'], 'L1_gnn_W': _L1_gnn_in['W'], 'L1_gnn_a': _L1_gnn_in['a']}

def reference(x, adj, L0_gnn_weight, L0_gnn_weight_a1, L0_gnn_weight_a2, L1_gnn_W, L1_gnn_a):
    import jax
    import jax.numpy as jnp

    def _L0_gnn_ref(xx, adj_hat, weight, weight_a1, weight_a2):
        import jax, jax.numpy as jnp
        import numpy as np
        N = 4096
        D_IN = 128
        D_OUT = 128
        ALPHA = 0.2
        h = jnp.matmul(xx, weight)
        f_1 = jnp.matmul(h, weight_a1)
        f_2 = jnp.matmul(h, weight_a2)
        e = jax.nn.leaky_relu(f_1 + f_2.T, negative_slope=ALPHA)
        masked = jnp.where(adj_hat > 0, e, -jnp.inf)
        attention = jax.nn.softmax(masked, axis=-1)
        h_prime = jnp.matmul(attention, h)
        return h_prime

    def _L1_gnn_ref(x, adj, W, a):
        import jax, jax.numpy as jnp
        import numpy as np
        N = 3072
        IN_DIM = 128
        OUT_DIM = 128
        NUM_HEADS = 4
        HEAD_DIM = OUT_DIM // NUM_HEADS
        NEG_SLOPE = 0.2
        n = x.shape[0]
        Wh = (x @ W).reshape(n, NUM_HEADS, HEAD_DIM)
        a_src, a_dst = (a[:HEAD_DIM], a[HEAD_DIM:])
        f_src = jnp.einsum('nhd,d->hn', Wh, a_src)
        f_dst = jnp.einsum('nhd,d->hn', Wh, a_dst)
        e = f_src[:, :, None] + f_dst[:, None, :]
        e = jnp.where(e > 0, e, NEG_SLOPE * e)
        mask = (adj != 0)[None, :, :]
        e = jnp.where(mask, e, -jnp.inf)
        alpha = jax.nn.softmax(e, axis=-1)
        alpha = jnp.nan_to_num(alpha, nan=0.0)
        out = jnp.einsum('hij,jhd->ihd', alpha, Wh).reshape(n, OUT_DIM)
        return out
    h = jnp.maximum(_layernorm(x, axis=-1), 0.0)
    x = x + _L0_gnn_ref(h, adj, L0_gnn_weight, L0_gnn_weight_a1, L0_gnn_weight_a2)
    h = jnp.maximum(_layernorm(x, axis=-1), 0.0)
    x = x + _L1_gnn_ref(h, adj, L1_gnn_W, L1_gnn_a)
    return x

_drawn_inputs = setup_inputs


def setup_inputs(seed=0):
    import zlib

    import numpy as np

    out = dict(_drawn_inputs(seed))
    spreads = {}
    factors = {}
    for name, (base, spread) in spreads.items():
        noise = np.random.default_rng([zlib.crc32(name.encode()), seed]).standard_normal(out[name].shape)
        drawn = base * np.exp(spread * noise) if base else spread * noise
        out[name] = jnp.asarray(drawn.astype(out[name].dtype))
    for name, factor in factors.items():
        out[name] = (out[name] * factor).astype(out[name].dtype)
    return out
```

```python
from contextlib import ExitStack

import concourse.bass as bass
from concourse import mybir

P = 128
D = 128
HEADS = (1, 4)
MAXH = max(HEADS)
F_DST = D
F_SRC = D + MAXH
GROW = D + MAXH
WIDTH = D + 2 * MAXH
FOUND = 8
CHUNKS = 8
RING = 4
QUARTERS = 4
PER_Q = CHUNKS // QUARTERS
SLOTS = 16
ALWAYS = 7
LAG = 4
SLOPE = 0.2
EPS = 1e-5
BIG = 1e30
MASKED = -1e30

ALU = mybir.AluOpType
ACT = mybir.ActivationFunctionType
F32 = mybir.dt.float32
I32 = mybir.dt.int32
U32 = mybir.dt.uint32
AX = mybir.AxisListType.X


class Count:

    def __init__(self):
        self.base = 0
        self.n = 0

    def inc(self):
        self.n += 1
        return self.base + self.n

    def now(self):
        return self.base + self.n


def build(nc, x, adj, w0, w0_a1, w0_a2, w1, a1h, out):
    N = x.shape[0]
    NT = N // P
    NG = NT // 2
    CH = N // CHUNKS
    QC = N // QUARTERS
    HD = D // HEADS[1]
    assert x.shape[1] == D and NG % 2 == 0 and NG >= LAG + 4 and LAG % 2 == 0

    tables = [nc.dram_tensor(f"table{layer}", [N, GROW], F32).ap() for layer in range(2)]
    x_pt = x.rearrange("(t p) d -> p t d", p=P)
    out_pt = out.rearrange("(t p) d -> p t d", p=P)
    table_pt = [t.rearrange("(t p) d -> p t d", p=P) for t in tables]
    adj_tq = adj.rearrange("(g s p) (q k c) -> g s q p k c", s=2, p=P, q=QUARTERS, k=PER_Q)

    with ExitStack() as ctx:
        def sb(name, shape, dt=F32):
            return ctx.enter_context(nc.sbuf_tensor(name, shape, dt))

        def bank(name):
            return ctx.enter_context(nc.psum_tensor(name, [P, 512], F32))

        def sem(name):
            return ctx.enter_context(nc.semaphore(name))

        ring = sb("ring", [P, RING, PER_Q, CH + FOUND], I32)
        x_sb = sb("x_sb", [P, NT, D])
        tab = sb("tab", [P, NT, WIDTH])
        gath = sb("gath", [P, 2, 2, SLOTS, GROW])
        idx_all = sb("idx_all", [P, NT, SLOTS], U32)
        idx_buf = [sb(f"idx_buf{b}", [P, 2 * SLOTS], U32) for b in range(2)]
        pen = sb("pen", [P, NT, SLOTS + 1])
        n_slots = sb("n_slots", [1, NT], I32)
        ident = sb("ident", [P, P])
        ones_i = sb("ones_i", [P, FOUND], I32)
        ones_f = sb("ones_f", [P, P])
        eps_col = sb("eps_col", [P, 1])
        chunk_base = sb("chunk_base", [P, 2, CHUNKS, FOUND])
        self_key = sb("self_key", [P, NT])
        w_ext = sb("w_ext", [P, 2, WIDTH])
        w_t = sb("w_t", [P, 2, D])
        a_cols = sb("a_cols", [P, 2, 2 * MAXH])
        h_sb = sb("h_sb", [P, 2, D])
        ht_sb = sb("ht_sb", [P, 2, D])
        found = sb("found", [P, 2, 2, CHUNKS, FOUND], U32)
        key = sb("key", [P, 2, CHUNKS * FOUND])
        cand = sb("cand", [P, 2, CHUNKS * FOUND])
        is_self = sb("is_self", [P, 2, CHUNKS * FOUND])
        self_flag = sb("self_flag", [P, NT])
        keys = sb("keys", [P, 2, SLOTS])
        last_found = sb("last_found", [P, 2, CHUNKS])
        cand_sum = sb("cand_sum", [P, NT])
        keys_sum = sb("keys_sum", [P, NT])
        used = sb("used", [1, 2, SLOTS])
        score = sb("score", [P, 2, MAXH, SLOTS + 1])
        top = sb("top", [P, 2, MAXH])
        total = sb("total", [P, 2, MAXH])
        inv = sb("inv", [P, 2, MAXH])
        prob = sb("prob", [P, 2, MAXH, SLOTS + 1])
        own = sb("own", [P, 2, D])
        stats = sb("stats", [P, 2, 6])
        stats_all = sb("stats_all", [P, NT, 6])
        mean_var = sb("mean_var", [P, 2, 2])
        var_all = sb("var_all", [P, NT])
        diff_all = sb("diff_all", [P, NT])
        std = sb("std", [P, NT])
        rstd = sb("rstd", [P, NT])
        shift = sb("shift", [P, NT])
        flags = sb("flags", [P, 4, NT])
        row_flag = sb("row_flag", [P, 4])
        any_flag = sb("any_flag", [P, 1])
        dense_flag = sb("dense_flag", [1, 1], I32)

        ps_t = bank("ps_t")
        ps_h = bank("ps_h")
        ps_n = bank("ps_n")
        ps_sum = [bank(f"ps_sum{b}") for b in range(2)]
        pt2 = ps_t[:, 0:2 * D].rearrange("p (s d) -> p s d", s=2)
        ph2 = ps_h[:, 0:2 * WIDTH].rearrange("p (s d) -> p s d", s=2)
        sum2 = [b[:, 0:2 * D].rearrange("p (s d) -> p s d", s=2) for b in ps_sum]

        x_loaded = sem("x_loaded")
        weights_loaded = sem("weights_loaded")
        a_loaded = sem("a_loaded")
        ident_ready = sem("ident_ready")
        consts_ready = sem("consts_ready")
        a_cleared = sem("a_cleared")
        dve_consts = sem("dve_consts")
        wt_in_psum = sem("wt_in_psum")
        wt_copied = sem("wt_copied")
        wa_in_psum = sem("wa_in_psum")
        w_ext_ready = sem("w_ext_ready")
        adj_landed = [sem(f"adj_landed{j}") for j in range(RING)]
        adj_scanned = sem("adj_scanned")
        vec_done = sem("vec_done")
        dve_passed = sem("dve_passed")
        var_ready = sem("var_ready")
        std_ready = sem("std_ready")
        ln_ready = sem("ln_ready")
        h_ready = sem("h_ready")
        ht_in_psum = sem("ht_in_psum")
        ht_copied = sem("ht_copied")
        hw_in_psum = sem("hw_in_psum")
        tab_ready = sem("tab_ready")
        table_stored = sem("table_stored")
        keys_ready = sem("keys_ready")
        used_in_psum = sem("used_in_psum")
        slots_counted = sem("slots_counted")
        idx_ready = sem("idx_ready")
        slot_landed = [sem(f"slot_landed{b}") for b in range(2)]
        rows_gathered = sem("rows_gathered")
        scores_ready = sem("scores_ready")
        exps_ready = sem("exps_ready")
        probs_ready = sem("probs_ready")
        weighted = sem("weighted")
        sums_ready = sem("sums_ready")
        x1_ready = sem("x1_ready")
        flag_in = sem("flag_in")
        flag_summed = sem("flag_summed")
        flag_ready = sem("flag_ready")
        out_stored = sem("out_stored")

        PARTS = ((0, 4), (4, 8), (8, 12), (12, 16), (16, 17))
        WPARTS = len(PARTS)

        def both(g):
            return bass.ds(2 * g, 2)

        def own_f(column, heads, g):
            return tab[:, both(g), column:column + heads]

        PASSES = [(layer, slice(h * (D // heads), (h + 1) * (D // heads)))
                  for layer, heads in enumerate(HEADS) for h in range(heads)]
        DENSE_STEPS = 8
        d_adj_int = ring[:, :, :, :].rearrange("p a b c -> p (a b c)")[:, 0:N]
        d_pen = d_adj_int.bitcast(F32)
        d_score = gath[:, :, :, :, :].rearrange("p a b c d -> p (a b c d)")[:, 0:N]
        d_f_dst = x_sb[:, :, :].rearrange("p t d -> p (t d)")
        adj_t = adj.rearrange("(t p) c -> t p c", p=P)
        d_top = sb("d_top", [P, 1])
        d_total = sb("d_total", [P, 1])
        d_adj_landed = sem("d_adj_landed")
        d_rest_landed = sem("d_rest_landed")
        d_diag_ready = sem("d_diag_ready")
        d_spread = sem("d_spread")
        d_scores_ready = sem("d_scores_ready")
        d_exps_ready = sem("d_exps_ready")
        d_probs_ready = sem("d_probs_ready")
        d_block_ready = sem("d_block_ready")
        d_turned = sem("d_turned")
        d_turned_copied = sem("d_turned_copied")
        d_sum_ready = sem("d_sum_ready")
        d_out_ready = sem("d_out_ready")
        pe_passed = sem("pe_passed")
        sp_passed = sem("sp_passed")

        block = ctx.enter_context(nc.Block())

        @block.sync
        def _(sp):
            sp.dma_start(w_ext[:, 0, 0:D], w0).then_inc(weights_loaded, 16)
            sp.dma_start(w_ext[:, 1, 0:D], w1).then_inc(weights_loaded, 16)
            sp.dma_start(x_sb[:, :, :], x_pt).then_inc(x_loaded, 16)

            def load_pair(g, first):
                for j in range(2 * QUARTERS):
                    slot = j % RING
                    if not (first and j < RING):
                        sp.wait_ge(adj_scanned, 2 * QUARTERS * g + j - RING + 1)
                    sp.dma_start(ring[:, slot, :, 0:CH],
                                 adj_tq[g, j // QUARTERS, j % QUARTERS]).then_inc(adj_landed[slot], 16)

            load_pair(0, True)
            with sp.Fori(1, NG) as g:
                load_pair(g, False)

            sp.wait_ge(flag_ready, 1)
            dense = sp.value_load(dense_flag[0:1, 0:1])
            with sp.If(dense > 0):
                for layer in range(2):
                    source = (x_pt, out_pt)[layer]
                    sp.dma_start(x_sb[:, :, :], source).then_inc(x_loaded, 16)
                    for n, (_, cols) in enumerate(PASSES):
                        if PASSES[n][0] != layer:
                            continue
                        with sp.Fori(0, NT) as t:
                            tile = n * NT + t
                            sp.dma_start(d_adj_int, adj_t[t]).then_inc(d_adj_landed, 16)
                            sp.dma_start(own[:, 1, 0:cols.stop - cols.start], source[:, bass.ds(t, 1), cols])\
                                .then_inc(d_rest_landed, 16)
                            sp.wait_ge(d_out_ready, tile + 1)
                            sp.sem_inc(sp_passed, 1)
                            sp.dma_start(out_pt[:, bass.ds(t, 1), cols], own[:, 0, 0:cols.stop - cols.start])\
                                .then_inc(out_stored, 16)
                            sp.wait_ge(out_stored, 16 * (tile + 1))
                            sp.sem_inc(sp_passed, 1)
            with sp.Else():
                with sp.Fori(0, NG) as g:
                    sp.wait_ge(x1_ready, NG + g + 1)
                    sp.dma_start(out_pt[:, both(g), :], x_sb[:, both(g), :]).then_inc(out_stored, 16)
                sp.wait_ge(out_stored, 16 * NG)

        @block.gpsimd
        def _(pool):
            nc.gpsimd.memset(a_cols[:, :, :], 0.0).then_inc(a_cleared, 1)
            nc.gpsimd.memset(ident[:, :], 0.0).then_inc(ident_ready, 1)
            pool.wait_ge(ident_ready, 1)
            nc.gpsimd.affine_select(out=ident[:, :], in_=ident[:, :], compare_op=ALU.not_equal, fill=1.0, base=0,
                                    pattern=[[-1, P]], channel_multiplier=1).then_inc(consts_ready, 1)
            nc.gpsimd.iota(chunk_base[:, :, :, :], [[0, 2], [-CH, CHUNKS], [0, FOUND]], base=N,
                           channel_multiplier=0, allow_small_or_imprecise_dtypes=True).then_inc(consts_ready, 1)
            nc.gpsimd.iota(self_key[:, :], [[-P, NT]], base=N, channel_multiplier=-1,
                           allow_small_or_imprecise_dtypes=True).then_inc(consts_ready, 1)

            landed = [pool.alloc_register(f"landed{b}") for b in range(2)]
            for b in range(2):
                pool.reg_mov(landed[b], 0)

            def pair_landed(b):
                pool.wait_ge(slot_landed[b], pool.snap(landed[b]))
                pool.sem_inc(rows_gathered, 1)

            def gather_pair(layer, g, b, buffer_used, previous):
                u = layer * NG + g
                pool.wait_ge(idx_ready, u + 1)
                if buffer_used:
                    pool.wait_ge(sums_ready, u - 1)
                if layer == 0:
                    pool.wait_ge(slots_counted, g + 1)
                pool.wait_ge(table_stored, 16 * NG * (layer + 1))
                slots = [pool.value_load(n_slots[0:1, bass.ds(2 * g + s, 1)]) for s in range(2)]
                for s in range(2):
                    for k in range(SLOTS):
                        if s == 0 and k == 2 and previous:
                            pair_landed(1 - b)

                        def gather():
                            nc.gpsimd.indirect_dma_start(
                                gath[:, b, s, k, :], None, tables[layer],
                                bass.IndirectOffsetOnAxis(ap=idx_buf[b][:, s * SLOTS + k:s * SLOTS + k + 1], axis=0),
                                bounds_check=N - 1, oob_is_err=False).then_inc(slot_landed[b], 16)
                            pool.reg_add(landed[b], landed[b], 16)

                        if k < ALWAYS:
                            gather()
                        else:
                            with pool.If(slots[s] > k):
                                gather()

            def gather_layer(layer):
                gather_pair(layer, 0, 0, layer > 0, False)
                gather_pair(layer, 1, 1, layer > 0, True)
                with pool.Fori(1, NG // 2) as d:
                    for b in range(2):
                        gather_pair(layer, 2 * d + b, b, True, True)
                pair_landed(1)

            gather_layer(0)
            pool.wait_ge(flag_ready, 1)
            dense = pool.value_load(dense_flag[0:1, 0:1])
            with pool.If(dense > 0):
                pool.wait_ge(flag_ready, 1)
            with pool.Else():
                gather_layer(1)

        @block.scalar
        def _(act):
            act.wait_ge(a_cleared, 1)
            act.dma_start(a_cols[:, 0, 0:1], w0_a2).then_inc(a_loaded, 16)
            act.dma_start(a_cols[:, 0, MAXH:MAXH + 1], w0_a1).then_inc(a_loaded, 16)
            for h in range(HEADS[1]):
                rows = slice(h * HD, (h + 1) * HD)
                act.dma_start(a_cols[rows, 1, h:h + 1], a1h[HD:2 * HD, :]).then_inc(a_loaded, 16)
                act.dma_start(a_cols[rows, 1, MAXH + h:MAXH + h + 1], a1h[0:HD, :]).then_inc(a_loaded, 16)
            act.wait_ge(wt_in_psum, 1)
            nc.scalar.activation(w_t[:, :, :], pt2, ACT.Copy).then_inc(wt_copied, 1)
            act.wait_ge(wa_in_psum, 1)
            nc.scalar.activation(w_ext[:, :, D:WIDTH], ph2[:, :, 0:2 * MAXH], ACT.Copy).then_inc(w_ext_ready, 1)

            act.wait_ge(var_ready, 1)
            act.wait_ge(dve_consts, 1)
            nc.scalar.activation(std[:, :], var_all[:, :], ACT.Sqrt, bias=eps_col[:, 0:1]).then_inc(std_ready, 1)

            def relu_pair(u, g, normed, peeled=False):
                act.wait_ge(ln_ready, normed)
                if not peeled:
                    act.wait_ge(ht_in_psum, u)
                for s in range(2):
                    t = bass.ds(2 * g + s, 1)
                    done = nc.scalar.activation(h_sb[:, s, :], x_sb[:, t, :], ACT.Relu, bias=shift[:, t],
                                                scale=rstd[:, t])
                done.then_inc(h_ready, 1)

            def copy_ht(u, peeled=False):
                act.wait_ge(ht_in_psum, u + 1)
                if not peeled:
                    act.wait_ge(hw_in_psum, u)
                nc.scalar.activation(ht_sb[:, :, :], pt2, ACT.Copy).then_inc(ht_copied, 1)

            def copy_table(u, g):
                act.wait_ge(hw_in_psum, u + 1)
                nc.scalar.activation(tab[:, both(g), :], ph2, ACT.Copy).then_inc(tab_ready, 1)

            def store_table(layer, g):
                act.wait_ge(tab_ready, layer * NG + g + 1)
                act.dma_start(table_pt[layer][:, both(g), :], tab[:, both(g), 0:GROW]).then_inc(table_stored, 16)

            relu_pair(0, 0, 1, True)
            copy_ht(0, True)
            relu_pair(1, 1, 1)
            copy_table(0, 0)
            with act.Fori(1, NG - 1) as g:
                copy_ht(g)
                relu_pair(g + 1, g + 1, 1)
                store_table(0, g - 1)
                copy_table(g, g)
            copy_ht(NG - 1)
            store_table(0, NG - 2)
            copy_table(NG - 1, NG - 1)
            store_table(0, NG - 1)

            def exps(layer, a):
                heads = HEADS[layer]
                act.wait_ge(scores_ready, layer * NG + a + 1)
                nc.scalar.activation(score[:, :, 0:heads, :], score[:, :, 0:heads, :], ACT.Exp).then_inc(exps_ready, 1)

            def weigh(a, b):
                act.wait_ge(probs_ready, a + 1)
                for s in range(2):
                    for first, end in PARTS:
                        for k in range(first, end):
                            rows = gath[:, b, s, k, 0:D] if k < SLOTS else None
                            if k < SLOTS:
                                done = nc.scalar.activation(rows, rows, ACT.Copy, scale=prob[:, s, 0, k:k + 1])
                            else:
                                done = nc.scalar.activation(own[:, s, :], tab[:, bass.ds(2 * a + s, 1), 0:D], ACT.Copy,
                                                            scale=prob[:, s, 0, k:k + 1])
                        done.then_inc(weighted, 1)

            def stream_step(a, b, steady):
                if steady or a >= 2:
                    relu_pair(NG + a - 2, a - 2, a)
                    copy_ht(NG + a - 2)
                    copy_table(NG + a - 2, a - 2)
                if steady or a < NG:
                    exps(0, a)
                    if steady or a >= 1:
                        act.wait_ge(sums_ready, a)
                    weigh(a, b)
                if steady or a >= 2:
                    store_table(1, a - 2)
                if steady or 1 <= a <= NG:
                    act.wait_ge(var_ready, a + 1)
                    nc.scalar.activation(std[:, 0:2], mean_var[:, :, 1], ACT.Sqrt, bias=eps_col[:, 0:1])\
                        .then_inc(std_ready, 1)

            for a in range(2):
                stream_step(a, a % 2, False)
            with act.Fori(1, NG // 2) as d:
                for b in range(2):
                    stream_step(2 * d + b, b, True)
            for a in range(NG, NG + 2):
                stream_step(a, a % 2, False)

            act.wait_ge(flag_ready, 1)
            dense = act.value_load(dense_flag[0:1, 0:1])
            with act.If(dense > 0):
                act.wait_ge(table_stored, 32 * NG)
                for layer in range(2):
                    act.wait_ge(var_ready, 1 + NG + layer + 1)
                    nc.scalar.activation(std[:, :], var_all[:, :], ACT.Sqrt, bias=eps_col[:, 0:1])\
                        .then_inc(std_ready, 1)
                    with act.Fori(0, NG) as g:
                        u = (2 + layer) * NG + g
                        relu_pair(u, g, 1 + NG + layer + 1)
                        copy_ht(u)
                        copy_table(u, g)
                    for n in range(len(PASSES)):
                        if PASSES[n][0] != layer:
                            continue
                        with act.Fori(0, NT) as t:
                            tile = n * NT + t
                            act.wait_ge(d_scores_ready, tile + 1)
                            nc.scalar.activation(d_score, d_score, ACT.Exp, bias=d_top[:, 0:1])\
                                .then_inc(d_exps_ready, 1)
            with act.Else():
                with act.Fori(0, NG) as a:
                    exps(1, a)

        @block.tensor
        def _(pe):
            pe.wait_ge(consts_ready, 3)
            pe.wait_ge(weights_loaded, 32)
            for layer in range(2):
                done = nc.tensor.transpose(pt2[:, layer, :], w_ext[:, layer, 0:D], ident[:, :])
            done.then_inc(wt_in_psum, 1)
            pe.wait_ge(wt_copied, 1)
            pe.wait_ge(a_loaded, 16 * (2 + 2 * HEADS[1]))
            for layer in range(2):
                done = nc.tensor.matmul(ph2[:, layer, 0:2 * MAXH], w_t[:, layer, :], a_cols[:, layer, :],
                                        start=True, stop=True)
            done.then_inc(wa_in_psum, 1)
            pe.wait_ge(w_ext_ready, 1)
            pe.wait_ge(dve_consts, 1)

            def turn(u, peeled=False):
                pe.wait_ge(h_ready, u + 1)
                if not peeled:
                    pe.wait_ge(ht_copied, u)
                for s in range(2):
                    done = nc.tensor.transpose(pt2[:, s, :], h_sb[:, s, :], ident[:, :])
                done.then_inc(ht_in_psum, 1)

            def project(layer, u, peeled=False):
                pe.wait_ge(ht_copied, u + 1)
                if not peeled:
                    pe.wait_ge(tab_ready, u)
                for s in range(2):
                    done = nc.tensor.matmul(ph2[:, s, :], ht_sb[:, s, :], w_ext[:, layer, :], start=True, stop=True)
                done.then_inc(hw_in_psum, 1)

            def sum_rows(layer, a, b, buffer_used):
                u = layer * NG + a
                if buffer_used:
                    pe.wait_ge(x1_ready, u - 1)
                for s in range(2):
                    for part, (first, end) in enumerate(PARTS):
                        pe.wait_ge(weighted, WPARTS * (2 * u + s) + part + 1)
                        for k in range(first, end):
                            rows = gath[:, b, s, k, 0:D] if k < SLOTS else own[:, s, :]
                            done = nc.tensor.matmul(sum2[b][:, s, :], ident[:, :], rows, start=(k == 0),
                                                    stop=(k == SLOTS))
                done.then_inc(sums_ready, 1)

            def count_used(g):
                pe.wait_ge(keys_ready, g + 1)
                nc.tensor.matmul(ps_n[0:1, 0:2 * SLOTS], ones_f[:, 0:1], keys[:, :, :], start=True, stop=True)\
                    .then_inc(used_in_psum, 1)

            turn(0, True)
            project(0, 0, True)
            with pe.Fori(1, NG) as g:
                turn(g)
                project(0, g)

            def stream_step(g, b, steady):
                if steady or g - LAG >= 2:
                    turn(NG + g - LAG - 2)
                    project(1, NG + g - LAG - 2)
                if steady or 0 <= g - LAG < NG:
                    sum_rows(0, g - LAG, b, steady or g - LAG >= 2)
                if steady or 1 <= g <= NG:
                    count_used(g - 1)

            for g in range(LAG + 2):
                stream_step(g, g % 2, False)
            with pe.Fori((LAG + 2) // 2, NG // 2) as d:
                for b in range(2):
                    stream_step(2 * d + b, b, True)
            for g in range(NG, NG + LAG + 2):
                stream_step(g, g % 2, False)

            pe.wait_ge(flag_in, 1)
            nc.tensor.matmul(ps_n[0:1, 64:65], ones_f[:, 0:1], any_flag[:, :], start=True, stop=True)\
                .then_inc(flag_summed, 1)
            pe.wait_ge(flag_ready, 1)
            dense = pe.value_load(dense_flag[0:1, 0:1])
            with pe.If(dense > 0):
                for layer in range(2):
                    with pe.Fori(0, NG) as g:
                        u = (2 + layer) * NG + g
                        turn(u)
                        project(layer, u)
                    for n, (_, cols) in enumerate(PASSES):
                        if PASSES[n][0] != layer:
                            continue
                        with pe.Fori(0, NT) as t:
                            pe.wait_ge(d_diag_ready, n * NT + t + 1)
                            nc.tensor.matmul(ps_h[:, 0:P], ones_f[:, :], h_sb[:, 0, :], start=True, stop=True)\
                                .then_inc(d_spread, 1)
                        with pe.Fori(0, NT) as t:
                            tile = n * NT + t

                            def block(j, first, last):
                                pe.wait_ge(d_block_ready, tile * NT + j + 1)
                                pe.sem_inc(pe_passed, 1)
                                nc.tensor.transpose(ps_t[:, 0:P], h_sb[:, 1, :], ident[:, :])\
                                    .then_inc(d_turned, 1)
                                pe.wait_ge(d_turned_copied, tile * NT + j + 1)
                                pe.sem_inc(pe_passed, 1)
                                return nc.tensor.matmul(ps_sum[0][:, 0:cols.stop - cols.start], ht_sb[:, 0, :],
                                                        tab[:, bass.ds(j, 1), cols], start=first, stop=last)

                            block(0, True, False)
                            with pe.Fori(1, NT - 1) as j:
                                block(j, False, False)
                            block(NT - 1, False, True).then_inc(d_sum_ready, 1)
            with pe.Else():
                with pe.Fori(0, NG // 2) as d:
                    for b in range(2):
                        sum_rows(1, 2 * d + b, b, True)

        @block.vector
        def _(dve):
            steps = Count()

            nc.vector.memset(ring[:, :, :, CH:CH + FOUND], 1)
            nc.vector.memset(ones_i[:, :], 1)
            nc.vector.memset(ones_f[:, :], 1.0)
            nc.vector.memset(last_found[:, :, :], float(N))
            nc.vector.memset(gath[:, :, :, :, :], 0.0)
            nc.vector.memset(eps_col[:, :], EPS).then_inc(dve_consts, 1)
            dve.wait_ge(dve_consts, 1)

            def norm_all(times, loads):
                dve.wait_ge(x_loaded, 16 * loads)
                with dve.Fori(0, NT) as t:
                    nc.vector.bn_stats(stats_all[:, bass.ds(t, 1), :], x_sb[:, bass.ds(t, 1), :]).then_inc(vec_done, 1)
                steps.n += NT
                dve.wait_ge(vec_done, steps.now())
                me, mo, ve, vo = (stats_all[:, :, i] for i in (1, 4, 2, 5))
                nc.vector.tensor_tensor(shift[:, :], me, mo, ALU.add)
                nc.vector.tensor_tensor(diff_all[:, :], me, mo, ALU.subtract).then_inc(vec_done, 1)
                nc.vector.tensor_tensor(var_all[:, :], ve, vo, ALU.add)
                dve.wait_ge(vec_done, steps.inc())
                nc.vector.scalar_tensor_tensor(diff_all[:, :], diff_all[:, :], 0.25, diff_all[:, :], ALU.mult,
                                               ALU.mult).then_inc(vec_done, 1)
                dve.wait_ge(vec_done, steps.inc())
                nc.vector.scalar_tensor_tensor(var_all[:, :], var_all[:, :], 1.0 / D, diff_all[:, :], ALU.mult,
                                               ALU.add).then_inc(var_ready, 1)
                dve.wait_ge(std_ready, times)
                nc.vector.reciprocal(rstd[:, :], std[:, :]).then_inc(vec_done, 1)
                dve.wait_ge(vec_done, steps.inc())
                nc.vector.scalar_tensor_tensor(shift[:, :], shift[:, :], -0.5, rstd[:, :], ALU.mult, ALU.mult)\
                    .then_inc(ln_ready, 1)
                dve.wait_ge(ln_ready, times)

            norm_all(1, 1)

            def scan(g, b, j):
                quarter, c = divmod(j, PER_Q)
                slot, s = quarter % RING, quarter // QUARTERS
                if c == 0:
                    dve.wait_ge(adj_landed[slot], 16 * (2 * QUARTERS // RING * g + quarter // RING + 1))
                    dve.sem_inc(dve_passed, 1)
                ins = nc.vector.max_index(found[:, b, s, j % CHUNKS, :], ones_i[:, :], ring[:, slot, c, :])
                if c == PER_Q - 1:
                    ins.then_inc(adj_scanned, 1)

            def add_parts(layer, a, b):
                heads = HEADS[layer]
                dve.wait_ge(rows_gathered, layer * NG + a + 1)
                f_src = own_f(F_SRC, heads, a)
                f_dst = gath[:, b, :, :, F_DST:F_DST + heads].rearrange("p s k h -> p s h k")
                nc.vector.tensor_tensor(score[:, :, 0:heads, 0:SLOTS], f_dst,
                                        f_src.unsqueeze(3).to_broadcast([P, 2, heads, SLOTS]), ALU.add)
                nc.vector.tensor_tensor(score[:, :, 0:heads, SLOTS], own_f(F_DST, heads, a), f_src, ALU.add)\
                    .then_inc(vec_done, 1)
                return steps.inc()

            def leaky(layer, after):
                e = score[:, :, 0:HEADS[layer], :]
                dve.wait_ge(vec_done, after)
                nc.vector.scalar_tensor_tensor(e, e, SLOPE, e, ALU.mult, ALU.max).then_inc(vec_done, 1)
                return steps.inc()

            def mask(layer, a, after):
                heads = HEADS[layer]
                e = score[:, :, 0:heads, :]
                dve.wait_ge(vec_done, after)
                nc.vector.tensor_tensor(e, e, pen[:, both(a), :].unsqueeze(2).to_broadcast([P, 2, heads, SLOTS + 1]),
                                        ALU.add).then_inc(vec_done, 1)
                return steps.inc()

            def row_max(layer, after):
                heads = HEADS[layer]
                dve.wait_ge(vec_done, after)
                nc.vector.tensor_reduce(top[:, :, 0:heads], score[:, :, 0:heads, :], AX, ALU.max).then_inc(vec_done, 1)
                return steps.inc()

            def minus_max(layer, after):
                heads = HEADS[layer]
                e = score[:, :, 0:heads, :]
                dve.wait_ge(vec_done, after)
                nc.vector.tensor_tensor(e, e, top[:, :, 0:heads].unsqueeze(3).to_broadcast([P, 2, heads, SLOTS + 1]),
                                        ALU.subtract).then_inc(scores_ready, 1)

            def row_total(layer, a):
                heads = HEADS[layer]
                dve.wait_ge(exps_ready, layer * NG + a + 1)
                nc.vector.tensor_reduce(total[:, :, 0:heads], score[:, :, 0:heads, :], AX, ALU.add)\
                    .then_inc(vec_done, 1)
                return steps.inc()

            def invert(layer, after):
                heads = HEADS[layer]
                dve.wait_ge(vec_done, after)
                nc.vector.reciprocal(inv[:, :, 0:heads], total[:, :, 0:heads]).then_inc(vec_done, 1)
                return steps.inc()

            def normalise(layer, a, after, buffer_used):
                heads = HEADS[layer]
                dve.wait_ge(vec_done, after)
                if buffer_used:
                    dve.wait_ge(weighted, 2 * WPARTS * (layer * NG + a))
                nc.vector.tensor_tensor(prob[:, :, 0:heads, :], score[:, :, 0:heads, :],
                                        inv[:, :, 0:heads].unsqueeze(3).to_broadcast([P, 2, heads, SLOTS + 1]),
                                        ALU.mult).then_inc(probs_ready, 1)

            def residual(layer, c, b):
                u = layer * NG + c
                dve.wait_ge(sums_ready, u + 1)
                rows = x_sb[:, both(c), :]
                nc.vector.tensor_tensor(rows, sum2[b], rows, ALU.add).then_inc(x1_ready, 1)

            def give_indices(layer, g, b):
                nc.vector.tensor_copy(idx_buf[b][:, :].rearrange("p (s k) -> p s k", s=2),
                                      idx_all[:, both(g), :]).then_inc(idx_ready, 1)

            def stream_step(g, b, steady):
                def has(pair):
                    return steady or 0 <= pair < NG

                a = g - LAG
                p = 1 - b
                scanning, listing, counting = steady or g < NG, has(g - 1), has(g - 2)
                attending, adding, norming = has(a), has(a - 1), has(a - 2)
                f = found[:, p].rearrange("p s c k -> p s (c k)")
                if attending:
                    after_add = add_parts(0, a, b)
                if scanning:
                    scan(g, b, 0)
                if attending:
                    after_leaky = leaky(0, after_add)
                if norming:
                    dve.wait_ge(std_ready, a)
                    nc.vector.reciprocal(rstd[:, both(a - 2)], std[:, 0:2]).then_inc(vec_done, 1)
                    after_rstd = steps.inc()
                if scanning:
                    scan(g, b, 1)
                if attending:
                    after_mask = mask(0, a, after_leaky)
                if norming:
                    dve.wait_ge(vec_done, after_rstd)
                    nc.vector.scalar_tensor_tensor(shift[:, both(a - 2)], mean_var[:, :, 0], -1.0,
                                                   rstd[:, both(a - 2)], ALU.mult, ALU.mult).then_inc(ln_ready, 1)
                if scanning:
                    scan(g, b, 2)
                if attending:
                    after_max = row_max(0, after_mask)
                if listing:
                    dve.wait_ge(adj_scanned, 2 * QUARTERS * g)
                    dve.wait_ge(consts_ready, 3)
                    nc.vector.tensor_tensor(key[:, :, :], chunk_base[:, :, :, :].rearrange("p s c k -> p s (c k)"),
                                            f, ALU.subtract).then_inc(vec_done, 1)
                    after_key = steps.inc()
                if scanning:
                    scan(g, b, 3)
                if attending:
                    minus_max(0, after_max)
                if listing:
                    dve.wait_ge(vec_done, after_key)
                    nc.vector.scalar_tensor_tensor(cand[:, :, :], f, float(CH), key[:, :, :], ALU.is_lt, ALU.mult)\
                        .then_inc(vec_done, 1)
                    after_cand = steps.inc()
                if counting:
                    dve.wait_ge(used_in_psum, g - 1)
                    nc.vector.tensor_scalar(used[:, :, :],
                                            ps_n[0:1, 0:2 * SLOTS].rearrange("p (s k) -> p s k", s=2),
                                            0.0, None, ALU.is_gt).then_inc(vec_done, 1)
                    after_used = steps.inc()
                if scanning:
                    scan(g, b, 4)
                if listing:
                    dve.wait_ge(vec_done, after_cand)
                    nc.vector.tensor_tensor(is_self[:, :, :], cand[:, :, :],
                                            self_key[:, both(g - 1)].unsqueeze(2)
                                            .to_broadcast([P, 2, CHUNKS * FOUND]), ALU.is_equal).then_inc(vec_done, 1)
                    after_self = steps.inc()
                    nc.vector.tensor_tensor(last_found[:, :, :], last_found[:, :, :],
                                            found[:, p, :, :, FOUND - 1], ALU.min).then_inc(vec_done, 1)
                    steps.inc()
                if counting:
                    dve.wait_ge(vec_done, after_used)
                    with nc.allow_low_precision(reason="counts up to SLOTS are exact"):
                        nc.vector.tensor_reduce(n_slots[0:1, both(g - 2)], used[:, :, :], AX, ALU.add)\
                            .then_inc(slots_counted, 1)
                if scanning:
                    scan(g, b, 5)
                if attending:
                    after_total = row_total(0, a)
                if listing:
                    dve.wait_ge(vec_done, after_self)
                    nc.vector.tensor_reduce(self_flag[:, both(g - 1)], is_self[:, :, :], AX, ALU.max)\
                        .then_inc(vec_done, 1)
                    after_flag = steps.inc()
                    nc.vector.scalar_tensor_tensor(cand[:, :, :], is_self[:, :, :], 0.0, cand[:, :, :],
                                                   ALU.is_equal, ALU.mult).then_inc(vec_done, 1)
                    after_others = steps.inc()
                if scanning:
                    scan(g, b, 6)
                if attending:
                    after_inv = invert(0, after_total)
                if listing:
                    dve.wait_ge(vec_done, after_others)
                    nc.vector.tensor_reduce(cand_sum[:, both(g - 1)], cand[:, :, :], AX, ALU.add)
                if scanning:
                    scan(g, b, 7)
                if attending:
                    normalise(0, a, after_inv, steady or a >= 1)
                if listing:
                    if steady or g >= 2:
                        dve.wait_ge(used_in_psum, g - 1)
                    dve.sem_inc(dve_passed, 1)
                    for s in range(2):
                        done = nc.vector.max(keys[:, s, 0:FOUND], cand[:, s, :])
                    done.then_inc(vec_done, 1)
                    after_first = steps.inc()
                if scanning:
                    scan(g, b, 8)
                if adding:
                    residual(0, a - 1, p)
                if listing:
                    dve.wait_ge(vec_done, after_first)
                    dve.sem_inc(dve_passed, 1)
                    for s in range(2):
                        done = nc.vector.match_replace(out=key[:, s, :], in_to_replace=keys[:, s, 0:FOUND],
                                                       in_values=cand[:, s, :], imm_value=0.0)
                    done.then_inc(vec_done, 1)
                    after_rest = steps.inc()
                if scanning:
                    scan(g, b, 9)
                if adding:
                    dve.wait_ge(x1_ready, a)
                    dve.sem_inc(dve_passed, 1)
                    for s in range(2):
                        done = nc.vector.bn_stats(stats[:, s, :], x_sb[:, bass.ds(2 * (a - 1) + s, 1), :])
                    done.then_inc(vec_done, 1)
                    after_stats = steps.inc()
                if listing:
                    dve.wait_ge(vec_done, after_rest)
                    dve.sem_inc(dve_passed, 1)
                    for s in range(2):
                        done = nc.vector.max(keys[:, s, FOUND:SLOTS], key[:, s, :])
                    done.then_inc(keys_ready, 1)
                if scanning:
                    scan(g, b, 10)
                if adding:
                    dve.wait_ge(vec_done, after_stats)
                    if norming:
                        dve.wait_ge(ln_ready, a)
                    dve.sem_inc(dve_passed, 1)
                    for s in range(2):
                        done = nc.vector.bn_aggr(mean_var[:, s, :], stats[:, s, :])
                    done.then_inc(var_ready, 1)
                if scanning:
                    scan(g, b, 11)
                if listing:
                    dve.wait_ge(keys_ready, g)
                    nc.vector.tensor_scalar(idx_all[:, both(g - 1), :], keys[:, :, :], -1.0, float(N), ALU.mult,
                                            ALU.add).then_inc(vec_done, 1)
                    steps.inc()
                    nc.vector.tensor_scalar(pen[:, both(g - 1), 0:SLOTS], keys[:, :, :], 0.0, MASKED, ALU.is_equal,
                                            ALU.mult).then_inc(vec_done, 1)
                    steps.inc()
                if scanning:
                    scan(g, b, 12)
                if listing:
                    dve.wait_ge(vec_done, after_flag)
                    nc.vector.tensor_scalar(pen[:, both(g - 1), SLOTS], self_flag[:, both(g - 1)], 0.0, MASKED,
                                            ALU.is_equal, ALU.mult).then_inc(vec_done, 1)
                    steps.inc()
                if scanning:
                    scan(g, b, 13)
                if listing:
                    nc.vector.tensor_reduce(keys_sum[:, both(g - 1)], keys[:, :, :], AX, ALU.add).then_inc(vec_done, 1)
                    steps.inc()
                if has(a + 2):
                    give_indices(0, a + 2, b)
                if scanning:
                    scan(g, b, 14)
                    scan(g, b, 15)

            for g in range(LAG + 2):
                stream_step(g, g % 2, False)
            before = steps.n
            with dve.Fori((LAG + 2) // 2, NG // 2) as d:
                STEPS = 21
                steps.base = before + (2 * d - (LAG + 2)) * STEPS
                steps.n = 0
                for b in range(2):
                    stream_step(2 * d + b, b, True)
                assert steps.n == 2 * STEPS, steps.n
            steps.base, steps.n = 0, before + (NG - LAG - 2) * STEPS
            for g in range(NG, NG + LAG + 2):
                stream_step(g, g % 2, False)

            dve.wait_ge(vec_done, steps.now())
            nc.vector.tensor_reduce(row_flag[:, 0:1], last_found[:, :, :].rearrange("p s c -> p (s c)"), AX, ALU.min)
            nc.vector.tensor_tensor(flags[:, 0, :], cand_sum[:, :], keys_sum[:, :], ALU.not_equal)
            nc.vector.tensor_tensor(flags[:, 1, :], pen[:, :, 0], pen[:, :, SLOTS], ALU.add).then_inc(vec_done, 1)
            dve.wait_ge(vec_done, steps.inc())
            nc.vector.tensor_scalar(row_flag[:, 2:3], row_flag[:, 0:1], float(CH), None, ALU.is_lt)
            nc.vector.tensor_reduce(row_flag[:, 1:2], flags[:, 0, :], AX, ALU.max)
            nc.vector.tensor_scalar(flags[:, 2, :], flags[:, 1, :], 1.5 * MASKED, None, ALU.is_lt)\
                .then_inc(vec_done, 1)
            dve.wait_ge(vec_done, steps.inc())
            nc.vector.tensor_reduce(row_flag[:, 3:4], flags[:, 2, :], AX, ALU.max).then_inc(vec_done, 1)
            dve.wait_ge(vec_done, steps.inc())
            nc.vector.tensor_reduce(any_flag[:, :], row_flag[:, 1:4], AX, ALU.max).then_inc(flag_in, 1)
            dve.wait_ge(flag_summed, 1)
            nc.vector.tensor_copy(dense_flag[0:1, 0:1], ps_n[0:1, 64:65]).then_inc(flag_ready, 1)
            dve.wait_ge(flag_ready, 1)

            def list_step(a, b, first, last):
                after = add_parts(1, a, b)
                if not last:
                    give_indices(1, a + 2, b)
                after = leaky(1, after)
                after = mask(1, a, after)
                after = row_max(1, after)
                minus_max(1, after)
                if not first:
                    residual(1, a - 1, 1 - b)
                after = row_total(1, a)
                after = invert(1, after)
                normalise(1, a, after, True)
                dve.wait_ge(probs_ready, NG + a + 1)
                for s in range(2):
                    for first_k, end in PARTS:
                        if first_k < SLOTS:
                            rows = gath[:, b, s, first_k:end, 0:D].rearrange("p k (h d) -> p k h d", h=HEADS[1])
                            w = prob[:, s, :, first_k:end].rearrange("p h k -> p k h")
                            nc.vector.tensor_tensor(rows, rows, w.unsqueeze(3)
                                                    .to_broadcast([P, end - first_k, HEADS[1], HD]), ALU.mult)\
                                .then_inc(weighted, 1)
                        else:
                            if s == 0:
                                dve.wait_ge(sums_ready, NG + a)
                            rows = tab[:, bass.ds(2 * a + s, 1), 0:D].rearrange("p o (h d) -> p (o h) d", h=HEADS[1])
                            w = prob[:, s, :, SLOTS]
                            nc.vector.tensor_tensor(own[:, s, :].rearrange("p (h d) -> p h d", h=HEADS[1]), rows,
                                                    w.unsqueeze(2).to_broadcast([P, HEADS[1], HD]), ALU.mult)\
                                .then_inc(weighted, 1)

            dense = dve.value_load(dense_flag[0:1, 0:1])
            listed = steps.n
            with dve.If(dense > 0):
                for layer in range(2):
                    norm_all(1 + NG + layer + 1, 2 + layer)
                    dve.wait_ge(tab_ready, (3 + layer) * NG)
                    for n, (_, cols) in enumerate(PASSES):
                        if PASSES[n][0] != layer:
                            continue
                        head = cols.start // (D // HEADS[layer])
                        width = cols.stop - cols.start
                        with dve.Fori(0, NT) as t:
                            k = n * NT + t
                            nc.vector.tensor_scalar(h_sb[:, 0, :], ident[:, :],
                                                    tab[:, bass.ds(t, 1), F_DST + head:F_DST + head + 1]
                                                    .rearrange("p o c -> p (o c)"), None, ALU.mult)\
                                .then_inc(d_diag_ready, 1)
                            dve.wait_ge(d_spread, k + 1)
                            nc.vector.tensor_scalar(d_f_dst[:, bass.ds(P * t, P)], ps_h[:, 0:P], 0.0, None, ALU.add)\
                                .then_inc(vec_done, 1)
                        steps.n += NT
                        dve.wait_ge(vec_done, steps.now())
                        before = steps.n
                        with dve.Fori(0, NT) as t:
                            tile = n * NT + t
                            steps.base, steps.n = before + t * DENSE_STEPS, 0
                            f_src = tab[:, bass.ds(t, 1), F_SRC + head:F_SRC + head + 1].rearrange("p o c -> p (o c)")
                            dve.wait_ge(d_adj_landed, 16 * (tile + 1))
                            nc.vector.tensor_scalar(d_pen, d_adj_int, 0.0, None, ALU.is_gt).then_inc(vec_done, 1)
                            dve.wait_ge(vec_done, steps.inc())
                            nc.vector.tensor_scalar(d_pen, d_pen, 1.0, BIG, ALU.subtract, ALU.mult)\
                                .then_inc(vec_done, 1)
                            steps.inc()
                            nc.vector.tensor_scalar(d_score, d_f_dst, f_src, None, ALU.add).then_inc(vec_done, 1)
                            dve.wait_ge(vec_done, steps.inc())
                            nc.vector.scalar_tensor_tensor(d_score, d_score, SLOPE, d_score, ALU.mult, ALU.max)\
                                .then_inc(vec_done, 1)
                            dve.wait_ge(vec_done, steps.inc())
                            nc.vector.tensor_tensor(d_score, d_score, d_pen, ALU.add).then_inc(vec_done, 1)
                            dve.wait_ge(vec_done, steps.inc())
                            nc.vector.tensor_reduce(d_top[:, :], d_score, AX, ALU.max).then_inc(vec_done, 1)
                            dve.wait_ge(vec_done, steps.inc())
                            nc.vector.tensor_scalar(d_top[:, :], d_top[:, :], -1.0, None, ALU.mult)\
                                .then_inc(d_scores_ready, 1)
                            dve.wait_ge(d_exps_ready, tile + 1)
                            nc.vector.scalar_tensor_tensor(d_score, d_pen, 0.0, d_score, ALU.is_equal, ALU.mult)\
                                .then_inc(d_probs_ready, 1)
                            dve.wait_ge(d_probs_ready, tile + 1)
                            nc.vector.tensor_reduce(d_total[:, :], d_score, AX, ALU.add).then_inc(vec_done, 1)
                            dve.wait_ge(vec_done, steps.inc())
                            nc.vector.reciprocal(d_total[:, :], d_total[:, :]).then_inc(vec_done, 1)
                            after_inv = steps.inc()
                            assert steps.n == DENSE_STEPS, steps.n
                            with dve.Fori(0, NT) as j:
                                nc.vector.tensor_copy(h_sb[:, 1, :], d_score[:, bass.ds(P * j, P)])\
                                    .then_inc(d_block_ready, 1)
                                dve.wait_ge(d_turned, tile * NT + j + 1)
                                nc.vector.tensor_copy(ht_sb[:, 0, :], ps_t[:, 0:P]).then_inc(d_turned_copied, 1)
                            dve.wait_ge(d_sum_ready, tile + 1)
                            dve.wait_ge(d_rest_landed, 16 * (tile + 1))
                            dve.wait_ge(vec_done, after_inv)
                            nc.vector.scalar_tensor_tensor(own[:, 0, 0:width], ps_sum[0][:, 0:width], d_total[:, 0:1],
                                                           own[:, 1, 0:width], ALU.mult, ALU.add)\
                                .then_inc(d_out_ready, 1)
                        steps.base, steps.n = 0, before + NT * DENSE_STEPS
            with dve.Else():
                steps.n = listed
                give_indices(1, 0, 0)
                give_indices(1, 1, 1)
                L1_STEPS = 6
                before = steps.n
                list_step(0, 0, True, False)
                list_step(1, 1, False, False)
                assert steps.n == before + 2 * L1_STEPS, steps.n - before
                before = steps.n
                with dve.Fori(1, NG // 2 - 1) as d:
                    steps.base = before + (2 * d - 2) * L1_STEPS
                    steps.n = 0
                    for b in range(2):
                        list_step(2 * d + b, b, False, False)
                steps.base, steps.n = 0, before + (NG - 4) * L1_STEPS
                list_step(NG - 2, 0, False, True)
                list_step(NG - 1, 1, False, True)
                residual(1, NG - 1, 1)


def kernel(x, adj, L0_gnn_weight, L0_gnn_weight_a1, L0_gnn_weight_a2, L1_gnn_W, L1_gnn_a):
    import numpy as np
    import concourse.bacc as bacc
    from concourse.bass_utils import run_bass_kernel_spmd

    nc = bacc.Bacc("TRN2", target_bir_lowering=False, num_devices=1)
    arrays = {
        "x": np.ascontiguousarray(x), "adj": np.ascontiguousarray(adj),
        "w0": np.ascontiguousarray(L0_gnn_weight), "w0_a1": np.ascontiguousarray(L0_gnn_weight_a1),
        "w0_a2": np.ascontiguousarray(L0_gnn_weight_a2), "w1": np.ascontiguousarray(L1_gnn_W),
        "a1h": np.ascontiguousarray(L1_gnn_a).reshape(-1, 1),
    }
    args = [nc.dram_tensor(n, a.shape, mybir.dt.from_np(a.dtype), kind="ExternalInput").ap()
            for n, a in arrays.items()]
    out = nc.dram_tensor("out", arrays["x"].shape, F32, kind="ExternalOutput").ap()
    build(nc, *args, out)
    r = run_bass_kernel_spmd(nc, [arrays], core_ids=[0])
    return r.results[0]["out"]
```

```python
from contextlib import ExitStack

import concourse.bass as bass
from concourse import mybir

P = 128
D = 128
HEADS = (1, 4)
MAXH = max(HEADS)
F_DST = D
F_SRC = D + MAXH
GROW = D + MAXH
WIDTH = D + 2 * MAXH
FOUND = 8
CHUNKS = 8
RING = 4
QUARTERS = 4
PER_Q = CHUNKS // QUARTERS
SLOTS = 16
DIRECT = 5
PACKED = SLOTS - DIRECT
GATHERS = DIRECT + 1
QUAD = 4
LAG = 4
SLOPE = 0.2
EPS = 1e-5
BIG = 1e30
MASKED = -1e30

ALU = mybir.AluOpType
ACT = mybir.ActivationFunctionType
F32 = mybir.dt.float32
I32 = mybir.dt.int32
U32 = mybir.dt.uint32
U8 = mybir.dt.uint8
AX = mybir.AxisListType.X


class Count:

    def __init__(self):
        self.base = 0
        self.n = 0

    def inc(self):
        self.n += 1
        return self.base + self.n

    def now(self):
        return self.base + self.n


def build(nc, x, adj, w0, w0_a1, w0_a2, w1, a1h, out):
    N = x.shape[0]
    NT = N // P
    NG = NT // 2
    CH = N // CHUNKS
    QC = N // QUARTERS
    HD = D // HEADS[1]
    NQ = NT // QUAD
    assert x.shape[1] == D and NG % 2 == 0 and NG > LAG + 4 and LAG % 2 == 0 and NQ > 4 and NQ % 2 == 0

    tables = [nc.dram_tensor(f"table{layer}", [N, GROW], F32).ap() for layer in range(2)]
    x_pt = x.rearrange("(t p) d -> p t d", p=P)
    out_pt = out.rearrange("(t p) d -> p t d", p=P)
    table_pt = [t.rearrange("(t p) d -> p t d", p=P) for t in tables]
    adj_tq = adj.rearrange("(g s p) (q k c) -> g s q p k c", s=2, p=P, q=QUARTERS, k=PER_Q)

    with ExitStack() as ctx:
        def sb(name, shape, dt=F32):
            return ctx.enter_context(nc.sbuf_tensor(name, shape, dt))

        def bank(name):
            return ctx.enter_context(nc.psum_tensor(name, [P, 512], F32))

        def sem(name):
            return ctx.enter_context(nc.semaphore(name))

        ring = sb("ring", [P, RING, PER_Q, CH + FOUND], I32)
        x_sb = sb("x_sb", [P, NT, D])
        tab = sb("tab", [P, NT, WIDTH])
        idx_all = sb("idx_all", [P, NT, GATHERS], U32)
        idx_buf = [sb(f"idx_buf{b}", [P, 2 * GATHERS], U32) for b in range(2)]
        pen = sb("pen", [P, NT, SLOTS + 1])
        place = sb("place", [P, NT, PACKED])

        gath_w, quad_w, pick_w = 4 * GATHERS * GROW, 2 * QUAD * D, NT * 2 * P // 4
        shared = sb("shared", [P, max(gath_w + 2 * quad_w + pick_w, N)])
        gath = shared[:, 0:gath_w].rearrange("p (b s k c) -> p b s k c", b=2, s=2, k=GATHERS)
        h_quad = shared[:, gath_w:gath_w + quad_w].rearrange("p (b s d) -> p b s d", b=2, s=QUAD)
        ht_quad = shared[:, gath_w + quad_w:gath_w + 2 * quad_w].rearrange("p (b s d) -> p b s d", b=2, s=QUAD)
        pick8 = shared[:, gath_w + 2 * quad_w:gath_w + 2 * quad_w + pick_w].bitcast(U8)\
            .rearrange("p (t w q) -> p t w q", t=NT, w=2)
        ident = sb("ident", [P, P])
        ones_i = sb("ones_i", [P, FOUND], I32)
        ones_f = sb("ones_f", [P, P])
        eps_col = sb("eps_col", [P, 1])
        chunk_base = sb("chunk_base", [P, 2, CHUNKS, FOUND])
        self_key = sb("self_key", [P, NT])
        w_ext = sb("w_ext", [P, 2, WIDTH])
        w_t = sb("w_t", [P, 2, D])
        a_cols = sb("a_cols", [P, 2, 2 * MAXH])
        h_sb = sb("h_sb", [P, 2, D])
        ht_sb = sb("ht_sb", [P, 2, D])
        found = sb("found", [P, 2, 2, CHUNKS, FOUND], U32)
        key = sb("key", [P, 2, CHUNKS * FOUND])
        cand = sb("cand", [P, 2, CHUNKS * FOUND])
        is_self = sb("is_self", [P, 2, CHUNKS * FOUND])
        self_flag = sb("self_flag", [P, NT])
        keys = sb("keys", [P, 2, SLOTS + 2])
        info = sb("info", [P, 2, PACKED + 2])
        tri = sb("tri", [P, P])
        iota_q = sb("iota_q", [P, P])
        iota_o = sb("iota_o", [P, P])
        col_q = sb("col_q", [P, 1])
        count = sb("count", [P, 2])
        has_packed = sb("has_packed", [P, 2, PACKED])
        below = sb("below", [P, 2, P], U8)
        end_all = sb("end_all", [P, NT])
        rank = sb("rank", [P, 2])
        own_key = sb("own_key", [P, 2, PACKED])
        packed_key = sb("packed_key", [P, 2])
        pick_map = sb("pick_map", [P, 2, P])
        pick = [sb(f"pick{b}", [P, 2, 2, P]) for b in range(2)]
        back = sb("back", [P, 2, PACKED, MAXH])
        packed_prob = sb("packed_prob", [P, 2, MAXH, PACKED])
        packed_w = sb("packed_w", [P, 2, MAXH])
        last_found = sb("last_found", [P, 2, CHUNKS])
        cand_sum = sb("cand_sum", [P, NT])
        keys_sum = sb("keys_sum", [P, NT])
        score = sb("score", [P, 2, MAXH, SLOTS + 1])
        top = sb("top", [P, 2, MAXH])
        total = sb("total", [P, 2, MAXH])
        inv = sb("inv", [P, 2, MAXH])
        prob = sb("prob", [P, 2, MAXH, SLOTS + 1])
        own = sb("own", [P, 2, D])
        stats = sb("stats", [P, 2, 6])
        stats_all = sb("stats_all", [P, NT, 6])
        mean_var = sb("mean_var", [P, 2, 2])
        var_all = sb("var_all", [P, NT])
        diff_all = sb("diff_all", [P, NT])
        std = sb("std", [P, NT])
        rstd = sb("rstd", [P, NT])
        shift = sb("shift", [P, NT])
        flags = sb("flags", [P, 4, NT])
        row_flag = sb("row_flag", [P, 5])
        any_flag = sb("any_flag", [P, 1])
        dense_flag = sb("dense_flag", [1, 1], I32)

        ps_t = [bank(f"ps_t{b}") for b in range(2)]
        ps_h = ctx.enter_context(nc.psum_tensor("ps_h", [P, 2, 512], F32))
        ps_sum = ctx.enter_context(nc.psum_tensor("ps_sum", [P, 2, 512], F32))
        ps_map = bank("ps_map")
        ps_move = bank("ps_move")
        pt2 = ps_t[0][:, 0:2 * D].rearrange("p (s d) -> p s d", s=2)
        ph2 = ps_h[:, 0, 0:2 * WIDTH].rearrange("p (s d) -> p s d", s=2)
        sum2 = [ps_sum[:, b, 0:2 * D].rearrange("p (s d) -> p s d", s=2) for b in range(2)]
        ps_offset = ps_map[:, 0:2]
        ps_info = ps_map[:, 16:16 + 2 * (PACKED + 2)].rearrange("p (s r) -> p s r", s=2)
        ps_flag = ps_map[0:1, 64:65]
        moved = PACKED * MAXH
        ps_back = ps_move[:, 0:2 * moved].rearrange("p (s r h) -> p s r h", s=2, h=MAXH)
        ps_prob = ps_move[:, 2 * moved:4 * moved].rearrange("p (s h r) -> p s h r", s=2, h=MAXH)

        x_loaded = sem("x_loaded")
        weights_loaded = sem("weights_loaded")
        a_loaded = sem("a_loaded")
        ident_ready = sem("ident_ready")
        consts_ready = sem("consts_ready")
        a_cleared = sem("a_cleared")
        dve_consts = sem("dve_consts")
        wt_in_psum = sem("wt_in_psum")
        wt_copied = sem("wt_copied")
        wa_in_psum = sem("wa_in_psum")
        w_ext_ready = sem("w_ext_ready")
        adj_landed = [sem(f"adj_landed{j}") for j in range(RING)]
        adj_scanned = sem("adj_scanned")
        vec_done = sem("vec_done")
        dve_passed = sem("dve_passed")
        var_ready = sem("var_ready")
        std_ready = sem("std_ready")
        ln_ready = sem("ln_ready")
        q_h_ready = sem("q_h_ready")
        q_ht_in_psum = sem("q_ht_in_psum")
        q_ht_copied = sem("q_ht_copied")
        q_hw_in_psum = sem("q_hw_in_psum")
        q_tab_ready = sem("q_tab_ready")
        h_ready = sem("h_ready")
        ht_in_psum = sem("ht_in_psum")
        ht_copied = sem("ht_copied")
        hw_in_psum = sem("hw_in_psum")
        tab_ready = sem("tab_ready")
        table_stored = sem("table_stored")
        keys_ready = sem("keys_ready")
        counts_ready = sem("counts_ready")
        offsets_in_psum = sem("offsets_in_psum")
        pick_ready = sem("pick_ready")
        pick_mapped = sem("pick_mapped")
        info_in_psum = sem("info_in_psum")
        places_ready = sem("places_ready")
        picks_loaded = sem("picks_loaded")
        idx_ready = sem("idx_ready")
        rows_landed = [sem(f"rows_landed{b}") for b in range(2)]
        back_ready = sem("back_ready")
        back_in_psum = sem("back_in_psum")
        prob_in_psum = sem("prob_in_psum")
        packed_w_ready = sem("packed_w_ready")
        scores_ready = sem("scores_ready")
        exps_ready = sem("exps_ready")
        probs_ready = sem("probs_ready")
        weighted = sem("weighted")
        packed_weighted = sem("packed_weighted")
        sums_ready = sem("sums_ready")
        x1_ready = sem("x1_ready")
        flag_in = sem("flag_in")
        flag_summed = sem("flag_summed")
        flag_ready = sem("flag_ready")
        out_stored = sem("out_stored")

        def both(g):
            return bass.ds(2 * g, 2)

        def own_f(column, heads, g):
            return tab[:, both(g), column:column + heads]

        PASSES = [(layer, slice(h * (D // heads), (h + 1) * (D // heads)))
                  for layer, heads in enumerate(HEADS) for h in range(heads)]
        DENSE_STEPS = 8
        d_adj_int = ring[:, :, :, :].rearrange("p a b c -> p (a b c)")[:, 0:N]
        d_pen = d_adj_int.bitcast(F32)
        d_score = shared[:, 0:N]
        d_f_dst = x_sb[:, :, :].rearrange("p t d -> p (t d)")
        adj_t = adj.rearrange("(t p) c -> t p c", p=P)
        d_top = sb("d_top", [P, 1])
        d_total = sb("d_total", [P, 1])
        d_adj_landed = sem("d_adj_landed")
        d_rest_landed = sem("d_rest_landed")
        d_diag_ready = sem("d_diag_ready")
        d_spread = sem("d_spread")
        d_scores_ready = sem("d_scores_ready")
        d_exps_ready = sem("d_exps_ready")
        d_probs_ready = sem("d_probs_ready")
        d_block_ready = sem("d_block_ready")
        d_turned = sem("d_turned")
        d_turned_copied = sem("d_turned_copied")
        d_sum_ready = sem("d_sum_ready")
        d_out_ready = sem("d_out_ready")
        pe_passed = sem("pe_passed")
        pool_passed = sem("pool_passed")
        act_passed = sem("act_passed")
        sp_passed = sem("sp_passed")

        N_CONSTS = 8

        block = ctx.enter_context(nc.Block())

        @block.sync
        def _(sp):
            sp.dma_start(w_ext[:, 0, 0:D], w0).then_inc(weights_loaded, 16)
            sp.dma_start(w_ext[:, 1, 0:D], w1).then_inc(weights_loaded, 16)
            sp.dma_start(x_sb[:, :, :], x_pt).then_inc(x_loaded, 16)

            def load_pair(g, first):
                for j in range(2 * QUARTERS):
                    slot = j % RING
                    if not (first and j < RING):
                        sp.wait_ge(adj_scanned, 2 * QUARTERS * g + j - RING + 1)
                    sp.dma_start(ring[:, slot, :, 0:CH],
                                 adj_tq[g, j // QUARTERS, j % QUARTERS]).then_inc(adj_landed[slot], 16)

            load_pair(0, True)
            with sp.Fori(1, NG) as g:
                load_pair(g, False)

            sp.wait_ge(flag_ready, 1)
            dense = sp.value_load(dense_flag[0:1, 0:1])
            with sp.If(dense > 0):
                for layer in range(2):
                    source = (x_pt, out_pt)[layer]
                    sp.dma_start(x_sb[:, :, :], source).then_inc(x_loaded, 16)
                    for n, (_, cols) in enumerate(PASSES):
                        if PASSES[n][0] != layer:
                            continue
                        with sp.Fori(0, NT) as t:
                            tile = n * NT + t
                            sp.dma_start(d_adj_int, adj_t[t]).then_inc(d_adj_landed, 16)
                            sp.dma_start(own[:, 1, 0:cols.stop - cols.start], source[:, bass.ds(t, 1), cols])\
                                .then_inc(d_rest_landed, 16)
                            sp.wait_ge(d_out_ready, tile + 1)
                            sp.sem_inc(sp_passed, 1)
                            sp.dma_start(out_pt[:, bass.ds(t, 1), cols], own[:, 0, 0:cols.stop - cols.start])\
                                .then_inc(out_stored, 16)
                            sp.wait_ge(out_stored, 16 * (tile + 1))
                            sp.sem_inc(sp_passed, 1)
            with sp.Else():
                with sp.Fori(0, NG) as g:
                    sp.wait_ge(x1_ready, NG + g + 1)
                    sp.dma_start(out_pt[:, both(g), :], x_sb[:, both(g), :]).then_inc(out_stored, 16)
                sp.wait_ge(out_stored, 16 * NG)

        @block.gpsimd
        def _(pool):
            nc.gpsimd.memset(a_cols[:, :, :], 0.0).then_inc(a_cleared, 1)
            nc.gpsimd.memset(ident[:, :], 0.0).then_inc(ident_ready, 1)
            pool.wait_ge(ident_ready, 1)
            nc.gpsimd.affine_select(out=ident[:, :], in_=ident[:, :], compare_op=ALU.not_equal, fill=1.0, base=0,
                                    pattern=[[-1, P]], channel_multiplier=1).then_inc(consts_ready, 1)
            nc.gpsimd.iota(chunk_base[:, :, :, :], [[0, 2], [-CH, CHUNKS], [0, FOUND]], base=N,
                           channel_multiplier=0, allow_small_or_imprecise_dtypes=True).then_inc(consts_ready, 1)
            nc.gpsimd.iota(self_key[:, :], [[-P, NT]], base=N, channel_multiplier=-1,
                           allow_small_or_imprecise_dtypes=True).then_inc(consts_ready, 1)

            nc.gpsimd.memset(tri[:, :], 1.0).then_inc(ident_ready, 1)
            pool.wait_ge(ident_ready, 2)
            nc.gpsimd.affine_select(out=tri[:, :], in_=tri[:, :], compare_op=ALU.is_gt, fill=0.0, base=0,
                                    pattern=[[1, P]], channel_multiplier=-1).then_inc(consts_ready, 1)
            nc.gpsimd.iota(iota_q[:, :], [[1, P]], base=0, channel_multiplier=0,
                           allow_small_or_imprecise_dtypes=True).then_inc(consts_ready, 1)
            nc.gpsimd.iota(iota_o[:, :], [[1, P]], base=1, channel_multiplier=0,
                           allow_small_or_imprecise_dtypes=True).then_inc(consts_ready, 1)
            nc.gpsimd.iota(col_q[:, :], [[0, 1]], base=0, channel_multiplier=1,
                           allow_small_or_imprecise_dtypes=True).then_inc(consts_ready, 1)
            nc.gpsimd.iota(keys[:, :, SLOTS + 1], [[0, 2]], base=1, channel_multiplier=1,
                           allow_small_or_imprecise_dtypes=True).then_inc(consts_ready, 1)

            def gather_pair(layer, g, b, buffer_used):
                u = layer * NG + g
                if buffer_used:
                    pool.wait_ge(sums_ready, u - 1)
                pool.wait_ge(idx_ready, u + 1)
                pool.sem_inc(pool_passed, 1)
                pool.wait_ge(table_stored, 16 * (NQ + layer * NG))
                for s in range(2):
                    for k in range(GATHERS):
                        at = s * GATHERS + k
                        nc.gpsimd.indirect_dma_start(
                            gath[:, b, s, k, :], None, tables[layer],
                            bass.IndirectOffsetOnAxis(ap=idx_buf[b][:, at:at + 1], axis=0),
                            bounds_check=N - 1, oob_is_err=False).then_inc(rows_landed[b], 16)

            def gather_layer(layer):
                for b in range(2):
                    gather_pair(layer, b, b, layer > 0)
                with pool.Fori(1, NG // 2) as d:
                    for b in range(2):
                        gather_pair(layer, 2 * d + b, b, True)

            gather_layer(0)
            pool.wait_ge(flag_ready, 1)
            dense = pool.value_load(dense_flag[0:1, 0:1])
            with pool.If(dense > 0):
                pool.wait_ge(flag_ready, 1)
            with pool.Else():
                gather_layer(1)

        @block.scalar
        def _(act):
            act.wait_ge(a_cleared, 1)
            act.dma_start(a_cols[:, 0, 0:1], w0_a2).then_inc(a_loaded, 16)
            act.dma_start(a_cols[:, 0, MAXH:MAXH + 1], w0_a1).then_inc(a_loaded, 16)
            for h in range(HEADS[1]):
                rows = slice(h * HD, (h + 1) * HD)
                act.dma_start(a_cols[rows, 1, h:h + 1], a1h[HD:2 * HD, :]).then_inc(a_loaded, 16)
                act.dma_start(a_cols[rows, 1, MAXH + h:MAXH + h + 1], a1h[0:HD, :]).then_inc(a_loaded, 16)
            act.wait_ge(wt_in_psum, 1)
            nc.scalar.activation(w_t[:, :, :], pt2, ACT.Copy).then_inc(wt_copied, 1)
            act.wait_ge(wa_in_psum, 1)
            nc.scalar.activation(w_ext[:, :, D:WIDTH], ph2[:, :, 0:2 * MAXH], ACT.Copy).then_inc(w_ext_ready, 1)

            act.wait_ge(var_ready, 1)
            act.wait_ge(dve_consts, 1)
            nc.scalar.activation(std[:, :], var_all[:, :], ACT.Sqrt, bias=eps_col[:, 0:1]).then_inc(std_ready, 1)

            def relu_pair(u, g, normed, peeled=False):
                act.wait_ge(ln_ready, normed)
                if not peeled:
                    act.wait_ge(ht_in_psum, u)
                for s in range(2):
                    t = bass.ds(2 * g + s, 1)
                    done = nc.scalar.activation(h_sb[:, s, :], x_sb[:, t, :], ACT.Relu, bias=shift[:, t],
                                                scale=rstd[:, t])
                done.then_inc(h_ready, 1)

            def copy_ht(u, peeled=False):
                act.wait_ge(ht_in_psum, u + 1)
                if not peeled:
                    act.wait_ge(hw_in_psum, u)
                nc.scalar.activation(ht_sb[:, :, :], pt2, ACT.Copy).then_inc(ht_copied, 1)

            def copy_table(u, g):
                act.wait_ge(hw_in_psum, u + 1)
                nc.scalar.activation(tab[:, both(g), :], ph2, ACT.Copy).then_inc(tab_ready, 1)

            def store_table(g):
                act.wait_ge(tab_ready, g + 1)
                act.dma_start(table_pt[1][:, both(g), :], tab[:, both(g), 0:GROW]).then_inc(table_stored, 16)

            def quad(q):
                return bass.ds(QUAD * q, QUAD)

            def quad_step(q, b, steady):
                if steady or q < NQ:
                    act.wait_ge(ln_ready, 1)
                    if steady or q >= 2:
                        act.wait_ge(q_ht_in_psum, q - 1)
                    for s in range(QUAD):
                        t = bass.ds(QUAD * q + s, 1)
                        done = nc.scalar.activation(h_quad[:, b, s, :], x_sb[:, t, :], ACT.Relu, bias=shift[:, t],
                                                    scale=rstd[:, t])
                    done.then_inc(q_h_ready, 1)
                if steady or 1 <= q <= NQ:
                    act.wait_ge(q_ht_in_psum, q)
                    if steady or q >= 3:
                        act.wait_ge(q_hw_in_psum, q - 2)
                    nc.scalar.activation(ht_quad[:, 1 - b, :, :],
                                         ps_t[1 - b][:, :].rearrange("p (s d) -> p s d", s=QUAD),
                                         ACT.Copy).then_inc(q_ht_copied, 1)
                if steady or q >= 3:
                    act.wait_ge(q_tab_ready, q - 2)
                    act.dma_start(table_pt[0][:, quad(q - 3), :], tab[:, quad(q - 3), 0:GROW])\
                        .then_inc(table_stored, 16)
                if steady or 2 <= q < NQ + 2:
                    act.wait_ge(q_hw_in_psum, q - 1)
                    banks = (ps_h, ps_sum)[b]
                    nc.scalar.activation(tab[:, quad(q - 2), :].rearrange("p (u s) w -> p u (s w)", u=2),
                                         banks[:, :, 0:2 * WIDTH], ACT.Copy).then_inc(q_tab_ready, 1)

            for q in range(4):
                quad_step(q, q % 2, False)
            with act.Fori(2, NQ // 2) as d:
                for b in range(2):
                    quad_step(2 * d + b, b, True)
            for q in range(NQ, NQ + 3):
                quad_step(q, q % 2, False)

            def load_picks(u, g, b, buffer_used):
                if buffer_used:
                    act.wait_ge(sums_ready, u - 1)
                    act.sem_inc(act_passed, 1)
                nc.scalar.activation(pick[b][:, :, :, :], pick8[:, both(g), :, :], ACT.Copy)\
                    .then_inc(picks_loaded, 1)

            def exps(layer, a):
                heads = HEADS[layer]
                act.wait_ge(scores_ready, layer * NG + a + 1)
                nc.scalar.activation(score[:, :, 0:heads, :], score[:, :, 0:heads, :], ACT.Exp).then_inc(exps_ready, 1)

            def weigh(a, b):
                act.wait_ge(probs_ready, a + 1)
                for s in range(2):
                    for k in range(DIRECT):
                        rows = gath[:, b, s, k, 0:D]
                        nc.scalar.activation(rows, rows, ACT.Copy, scale=prob[:, s, 0, k:k + 1])
                    nc.scalar.activation(own[:, s, :], tab[:, bass.ds(2 * a + s, 1), 0:D], ACT.Copy,
                                         scale=prob[:, s, 0, SLOTS:SLOTS + 1]).then_inc(weighted, 1)
                act.wait_ge(packed_w_ready, a + 1)
                for s in range(2):
                    rows = gath[:, b, s, DIRECT, 0:D]
                    nc.scalar.activation(rows, rows, ACT.Copy, scale=packed_w[:, s, 0:1])\
                        .then_inc(packed_weighted, 1)

            def map_pick(m):
                act.wait_ge(pick_ready, m + 1)
                act.sem_inc(act_passed, 1)
                nc.scalar.activation(pick_map[:, :, :], pick8[:, both(m), 0, :], ACT.Copy).then_inc(pick_mapped, 1)

            def stream_step(g, b, steady):
                a = g - LAG
                if steady or a >= 2:
                    relu_pair(a - 2, a - 2, a, not steady and a == 2)
                    copy_ht(a - 2, not steady and a == 2)
                    copy_table(a - 2, a - 2)
                if steady or 2 <= g < NG + 2:
                    map_pick(g - 2)
                if steady or 0 <= a < NG:
                    exps(0, a)
                    if steady or a >= 1:
                        act.wait_ge(sums_ready, a)
                    weigh(a, b)
                if steady or a >= 2:
                    store_table(a - 2)
                if steady or 1 <= a <= NG:
                    act.wait_ge(var_ready, a + 1)
                    nc.scalar.activation(std[:, 0:2], mean_var[:, :, 1], ACT.Sqrt, bias=eps_col[:, 0:1])\
                        .then_inc(std_ready, 1)
                if steady or 0 <= a + 1 < NG:
                    if not steady:
                        act.wait_ge(places_ready, a + 2)
                    load_picks(a + 1, a + 1, 1 - b, steady or a + 1 >= 2)

            for g in range(2, LAG + 4):
                stream_step(g, g % 2, False)
            with act.Fori((LAG + 4) // 2, NG // 2) as d:
                for b in range(2):
                    stream_step(2 * d + b, b, True)
            for g in range(NG, NG + LAG + 2):
                stream_step(g, g % 2, False)

            act.wait_ge(flag_ready, 1)
            dense = act.value_load(dense_flag[0:1, 0:1])
            with act.If(dense > 0):
                act.wait_ge(table_stored, 16 * (NQ + NG))
                for layer in range(2):
                    act.wait_ge(var_ready, 1 + NG + layer + 1)
                    nc.scalar.activation(std[:, :], var_all[:, :], ACT.Sqrt, bias=eps_col[:, 0:1])\
                        .then_inc(std_ready, 1)
                    with act.Fori(0, NG) as g:
                        u = (1 + layer) * NG + g
                        relu_pair(u, g, 1 + NG + layer + 1)
                        copy_ht(u)
                        copy_table(u, g)
                    for n in range(len(PASSES)):
                        if PASSES[n][0] != layer:
                            continue
                        with act.Fori(0, NT) as t:
                            tile = n * NT + t
                            act.wait_ge(d_scores_ready, tile + 1)
                            nc.scalar.activation(d_score, d_score, ACT.Exp, bias=d_top[:, 0:1])\
                                .then_inc(d_exps_ready, 1)
            with act.Else():
                load_picks(NG, 0, 0, True)
                with act.Fori(0, NG // 2 - 1) as d:
                    for b in range(2):
                        exps(1, 2 * d + b)
                        load_picks(NG + 2 * d + b + 1, 2 * d + b + 1, 1 - b, True)
                exps(1, NG - 2)
                load_picks(2 * NG - 1, NG - 1, 1, True)
                exps(1, NG - 1)

        @block.tensor
        def _(pe):
            pe.wait_ge(consts_ready, N_CONSTS)
            pe.wait_ge(weights_loaded, 32)
            for layer in range(2):
                done = nc.tensor.transpose(pt2[:, layer, :], w_ext[:, layer, 0:D], ident[:, :])
            done.then_inc(wt_in_psum, 1)
            pe.wait_ge(wt_copied, 1)
            pe.wait_ge(a_loaded, 16 * (2 + 2 * HEADS[1]))
            for layer in range(2):
                done = nc.tensor.matmul(ph2[:, layer, 0:2 * MAXH], w_t[:, layer, :], a_cols[:, layer, :],
                                        start=True, stop=True)
            done.then_inc(wa_in_psum, 1)
            pe.wait_ge(w_ext_ready, 1)
            pe.wait_ge(dve_consts, 1)

            def turn(u, peeled=False):
                pe.wait_ge(h_ready, u + 1)
                if not peeled:
                    pe.wait_ge(ht_copied, u)
                for s in range(2):
                    done = nc.tensor.transpose(pt2[:, s, :], h_sb[:, s, :], ident[:, :])
                done.then_inc(ht_in_psum, 1)

            def project(layer, u, peeled=False):
                pe.wait_ge(ht_copied, u + 1)
                if not peeled:
                    pe.wait_ge(tab_ready, u)
                for s in range(2):
                    done = nc.tensor.matmul(ph2[:, s, :], ht_sb[:, s, :], w_ext[:, layer, :], start=True, stop=True)
                done.then_inc(hw_in_psum, 1)

            def send_back(u, b, heads):
                pe.wait_ge(picks_loaded, u + 1)
                pe.wait_ge(back_ready, u + 1)
                for s in range(2):
                    done = nc.tensor.matmul(ps_back[:, s, :, 0:heads], pick[b][:, s, 1, :], back[:, s, :, 0:heads],
                                            start=True, stop=True)
                done.then_inc(back_in_psum, 1)

            def send_probs(u, b, heads):
                pe.wait_ge(probs_ready, u + 1)
                for s in range(2):
                    done = nc.tensor.matmul(ps_prob[:, s, 0:heads, :], pick[b][:, s, 0, :],
                                            prob[:, s, 0:heads, DIRECT:SLOTS], start=True, stop=True)
                done.then_inc(prob_in_psum, 1)

            def sum_rows(u, b, buffer_used):
                if buffer_used:
                    pe.wait_ge(x1_ready, u - 1)
                for s in range(2):
                    pe.wait_ge(weighted, 2 * u + s + 1)
                    for k in range(DIRECT):
                        nc.tensor.matmul(sum2[b][:, s, :], ident[:, :], gath[:, b, s, k, 0:D], start=(k == 0),
                                         stop=False)
                    nc.tensor.matmul(sum2[b][:, s, :], ident[:, :], own[:, s, :], start=False, stop=False)
                    pe.wait_ge(packed_weighted, 2 * u + s + 1)
                    done = nc.tensor.matmul(sum2[b][:, s, :], pick[b][:, s, 1, :], gath[:, b, s, DIRECT, 0:D],
                                            start=False, stop=True)
                done.then_inc(sums_ready, 1)

            def offsets(l):
                pe.wait_ge(counts_ready, l + 1)
                nc.tensor.matmul(ps_offset, tri[:, :], count[:, :], start=True, stop=True)\
                    .then_inc(offsets_in_psum, 1)

            def owner_info(m):
                pe.wait_ge(pick_mapped, m + 1)
                for s in range(2):
                    done = nc.tensor.matmul(ps_info[:, s, :], pick_map[:, s, :], keys[:, s, DIRECT:], start=True,
                                            stop=True)
                done.then_inc(info_in_psum, 1)

            def quad_step(q, b, steady):
                if steady or q < NQ:
                    pe.wait_ge(q_h_ready, q + 1)
                    if steady or q >= 2:
                        pe.wait_ge(q_ht_copied, q - 1)
                    for s in range(QUAD):
                        done = nc.tensor.transpose(ps_t[b][:, s * D:(s + 1) * D], h_quad[:, b, s, :], ident[:, :])
                    done.then_inc(q_ht_in_psum, 1)
                if steady or 1 <= q:
                    pe.wait_ge(q_ht_copied, q)
                    if steady or q >= 3:
                        pe.wait_ge(q_tab_ready, q - 2)
                    banks = (ps_h, ps_sum)[1 - b]
                    for s in range(QUAD):
                        done = nc.tensor.matmul(banks[:, s // 2, s % 2 * WIDTH:(s % 2 + 1) * WIDTH],
                                                ht_quad[:, 1 - b, s, :], w_ext[:, 0, :], start=True, stop=True)
                    done.then_inc(q_hw_in_psum, 1)

            for q in range(4):
                quad_step(q, q % 2, False)
            with pe.Fori(2, NQ // 2) as d:
                for b in range(2):
                    quad_step(2 * d + b, b, True)
            quad_step(NQ, 0, False)
            pe.wait_ge(q_tab_ready, NQ)

            def stream_step(g, b, steady):
                a = g - LAG
                if steady or 0 <= a < NG:
                    send_back(a, b, 1)
                if steady or a >= 2:
                    turn(a - 2, not steady and a == 2)
                    project(1, a - 2, not steady and a == 2)
                if steady or 2 <= g < NG + 2:
                    owner_info(g - 2)
                if steady or 0 <= a < NG:
                    send_probs(a, b, 1)
                    sum_rows(a, b, steady or a >= 2)
                if steady or 1 <= g <= NG:
                    offsets(g - 1)

            for g in range(1, LAG + 4):
                stream_step(g, g % 2, False)
            with pe.Fori((LAG + 4) // 2, NG // 2) as d:
                for b in range(2):
                    stream_step(2 * d + b, b, True)
            for g in range(NG, NG + LAG + 2):
                stream_step(g, g % 2, False)

            pe.wait_ge(flag_in, 1)
            nc.tensor.matmul(ps_flag, ones_f[:, 0:1], any_flag[:, :], start=True, stop=True)\
                .then_inc(flag_summed, 1)
            pe.wait_ge(flag_ready, 1)
            dense = pe.value_load(dense_flag[0:1, 0:1])
            with pe.If(dense > 0):
                for layer in range(2):
                    with pe.Fori(0, NG) as g:
                        u = (1 + layer) * NG + g
                        turn(u)
                        project(layer, u)
                    for n, (_, cols) in enumerate(PASSES):
                        if PASSES[n][0] != layer:
                            continue
                        with pe.Fori(0, NT) as t:
                            pe.wait_ge(d_diag_ready, n * NT + t + 1)
                            nc.tensor.matmul(ps_h[:, 0, 0:P], ones_f[:, :], h_sb[:, 0, :], start=True, stop=True)\
                                .then_inc(d_spread, 1)
                        with pe.Fori(0, NT) as t:
                            tile = n * NT + t

                            def block(j, first, last):
                                pe.wait_ge(d_block_ready, tile * NT + j + 1)
                                pe.sem_inc(pe_passed, 1)
                                nc.tensor.transpose(ps_t[0][:, 0:P], h_sb[:, 1, :], ident[:, :])\
                                    .then_inc(d_turned, 1)
                                pe.wait_ge(d_turned_copied, tile * NT + j + 1)
                                pe.sem_inc(pe_passed, 1)
                                return nc.tensor.matmul(ps_sum[:, 0, 0:cols.stop - cols.start], ht_sb[:, 0, :],
                                                        tab[:, bass.ds(j, 1), cols], start=first, stop=last)

                            block(0, True, False)
                            with pe.Fori(1, NT - 1) as j:
                                block(j, False, False)
                            block(NT - 1, False, True).then_inc(d_sum_ready, 1)
            with pe.Else():
                with pe.Fori(0, NG // 2) as d:
                    for b in range(2):
                        u = NG + 2 * d + b
                        send_back(u, b, HEADS[1])
                        send_probs(u, b, HEADS[1])
                        sum_rows(u, b, True)

        @block.vector
        def _(dve):
            steps = Count()

            nc.vector.memset(ring[:, :, :, CH:CH + FOUND], 1)
            nc.vector.memset(ones_i[:, :], 1)
            nc.vector.memset(ones_f[:, :], 1.0)
            nc.vector.memset(last_found[:, :, :], float(N))
            nc.vector.memset(gath, 0.0)
            nc.vector.memset(eps_col[:, :], EPS).then_inc(dve_consts, 1)
            dve.wait_ge(dve_consts, 1)

            def norm_all(times, loads):
                dve.wait_ge(x_loaded, 16 * loads)
                with dve.Fori(0, NT) as t:
                    nc.vector.bn_stats(stats_all[:, bass.ds(t, 1), :], x_sb[:, bass.ds(t, 1), :]).then_inc(vec_done, 1)
                steps.n += NT
                dve.wait_ge(vec_done, steps.now())
                me, mo, ve, vo = (stats_all[:, :, i] for i in (1, 4, 2, 5))
                nc.vector.tensor_tensor(shift[:, :], me, mo, ALU.add)
                nc.vector.tensor_tensor(diff_all[:, :], me, mo, ALU.subtract).then_inc(vec_done, 1)
                nc.vector.tensor_tensor(var_all[:, :], ve, vo, ALU.add)
                dve.wait_ge(vec_done, steps.inc())
                nc.vector.scalar_tensor_tensor(diff_all[:, :], diff_all[:, :], 0.25, diff_all[:, :], ALU.mult,
                                               ALU.mult).then_inc(vec_done, 1)
                dve.wait_ge(vec_done, steps.inc())
                nc.vector.scalar_tensor_tensor(var_all[:, :], var_all[:, :], 1.0 / D, diff_all[:, :], ALU.mult,
                                               ALU.add).then_inc(var_ready, 1)
                dve.wait_ge(std_ready, times)
                nc.vector.reciprocal(rstd[:, :], std[:, :]).then_inc(vec_done, 1)
                dve.wait_ge(vec_done, steps.inc())
                nc.vector.scalar_tensor_tensor(shift[:, :], shift[:, :], -0.5, rstd[:, :], ALU.mult, ALU.mult)\
                    .then_inc(ln_ready, 1)
                dve.wait_ge(ln_ready, times)

            norm_all(1, 1)

            def scan(g, b, j):
                quarter, c = divmod(j, PER_Q)
                slot, s = quarter % RING, quarter // QUARTERS
                if c == 0:
                    dve.wait_ge(adj_landed[slot], 16 * (2 * QUARTERS // RING * g + quarter // RING + 1))
                    dve.sem_inc(dve_passed, 1)
                ins = nc.vector.max_index(found[:, b, s, j % CHUNKS, :], ones_i[:, :], ring[:, slot, c, :])
                if c == PER_Q - 1:
                    ins.then_inc(adj_scanned, 1)

            def put_back(layer, a, b):
                heads = HEADS[layer]
                dve.wait_ge(rows_landed[b], 16 * 2 * GATHERS * ((layer * NG + a - b) // 2 + 1))
                f_dst = gath[:, b, :, DIRECT, F_DST:F_DST + heads]
                nc.vector.tensor_tensor(back[:, :, :, 0:heads],
                                        place[:, both(a), :].unsqueeze(3).to_broadcast([P, 2, PACKED, heads]),
                                        f_dst.unsqueeze(2).to_broadcast([P, 2, PACKED, heads]), ALU.mult)\
                    .then_inc(back_ready, 1)

            def add_direct(layer, a, b):
                heads = HEADS[layer]
                f_src = own_f(F_SRC, heads, a)
                f_dst = gath[:, b, :, 0:DIRECT, F_DST:F_DST + heads].rearrange("p s k h -> p s h k")
                nc.vector.tensor_tensor(score[:, :, 0:heads, 0:DIRECT], f_dst,
                                        f_src.unsqueeze(3).to_broadcast([P, 2, heads, DIRECT]), ALU.add)
                nc.vector.tensor_tensor(score[:, :, 0:heads, SLOTS], own_f(F_DST, heads, a), f_src, ALU.add)

            def add_packed(layer, a):
                heads = HEADS[layer]
                dve.wait_ge(back_in_psum, layer * NG + a + 1)
                f_dst = ps_back[:, :, :, 0:heads].rearrange("p s r h -> p s h r")
                nc.vector.tensor_tensor(score[:, :, 0:heads, DIRECT:SLOTS], f_dst,
                                        own_f(F_SRC, heads, a).unsqueeze(3).to_broadcast([P, 2, heads, PACKED]),
                                        ALU.add).then_inc(vec_done, 1)
                return steps.inc()

            def leaky(layer, after):
                e = score[:, :, 0:HEADS[layer], :]
                dve.wait_ge(vec_done, after)
                nc.vector.scalar_tensor_tensor(e, e, SLOPE, e, ALU.mult, ALU.max).then_inc(vec_done, 1)
                return steps.inc()

            def mask(layer, a, after):
                heads = HEADS[layer]
                e = score[:, :, 0:heads, :]
                dve.wait_ge(vec_done, after)
                nc.vector.tensor_tensor(e, e, pen[:, both(a), :].unsqueeze(2).to_broadcast([P, 2, heads, SLOTS + 1]),
                                        ALU.add).then_inc(vec_done, 1)
                return steps.inc()

            def row_max(layer, after):
                heads = HEADS[layer]
                dve.wait_ge(vec_done, after)
                nc.vector.tensor_reduce(top[:, :, 0:heads], score[:, :, 0:heads, :], AX, ALU.max).then_inc(vec_done, 1)
                return steps.inc()

            def minus_max(layer, after):
                heads = HEADS[layer]
                e = score[:, :, 0:heads, :]
                dve.wait_ge(vec_done, after)
                nc.vector.tensor_tensor(e, e, top[:, :, 0:heads].unsqueeze(3).to_broadcast([P, 2, heads, SLOTS + 1]),
                                        ALU.subtract).then_inc(scores_ready, 1)

            def row_total(layer, a):
                heads = HEADS[layer]
                dve.wait_ge(exps_ready, layer * NG + a + 1)
                nc.vector.tensor_reduce(total[:, :, 0:heads], score[:, :, 0:heads, :], AX, ALU.add)\
                    .then_inc(vec_done, 1)
                return steps.inc()

            def invert(layer, after):
                heads = HEADS[layer]
                dve.wait_ge(vec_done, after)
                nc.vector.reciprocal(inv[:, :, 0:heads], total[:, :, 0:heads]).then_inc(vec_done, 1)
                return steps.inc()

            def normalise(layer, a, after, buffer_used):
                heads = HEADS[layer]
                dve.wait_ge(vec_done, after)
                if buffer_used:
                    dve.wait_ge(weighted, 2 * (layer * NG + a))
                nc.vector.tensor_tensor(prob[:, :, 0:heads, :], score[:, :, 0:heads, :],
                                        inv[:, :, 0:heads].unsqueeze(3).to_broadcast([P, 2, heads, SLOTS + 1]),
                                        ALU.mult).then_inc(probs_ready, 1)

            def place_probs(layer, a):
                heads = HEADS[layer]
                dve.wait_ge(prob_in_psum, layer * NG + a + 1)
                at = place[:, both(a), :].unsqueeze(2).to_broadcast([P, 2, heads, PACKED])
                nc.vector.tensor_tensor(packed_prob[:, :, 0:heads, :], ps_prob[:, :, 0:heads, :], at, ALU.mult)\
                    .then_inc(vec_done, 1)
                return steps.inc()

            def packed_weights(layer, a, after):
                heads = HEADS[layer]
                dve.wait_ge(vec_done, after)
                if layer == 0:
                    if not isinstance(a, int) or a > 0:
                        dve.wait_ge(packed_weighted, 2 * a)
                nc.vector.tensor_reduce(packed_w[:, :, 0:heads], packed_prob[:, :, 0:heads, :], AX, ALU.add)\
                    .then_inc(packed_w_ready, 1)

            def residual(layer, c, b):
                u = layer * NG + c
                dve.wait_ge(sums_ready, u + 1)
                rows = x_sb[:, both(c), :]
                nc.vector.tensor_tensor(rows, sum2[b], rows, ALU.add).then_inc(x1_ready, 1)

            def give_indices(layer, g, b):
                nc.vector.tensor_copy(idx_buf[b][:, :].rearrange("p (s k) -> p s k", s=2),
                                      idx_all[:, both(g), :]).then_inc(idx_ready, 1)

            def stream_step(g, b, steady):
                def has(pair):
                    return steady or 0 <= pair < NG

                a = g - LAG
                p = 1 - b
                scanning, listing, packing = steady or g < NG, has(g - 1), has(g - 2)
                attending, adding, norming = has(a), has(a - 1), has(a - 2)
                f = found[:, p].rearrange("p s c k -> p s (c k)")
                if attending:
                    put_back(0, a, b)
                    add_direct(0, a, b)
                if scanning:
                    scan(g, b, 0)
                if packing:
                    dve.wait_ge(offsets_in_psum, g - 1)
                    nc.vector.tensor_copy(keys[:, :, SLOTS], ps_offset).then_inc(vec_done, 1)
                    after_offset = steps.inc()
                    nc.vector.tensor_tensor(end_all[:, both(g - 2)], ps_offset, count[:, :], ALU.add)\
                        .then_inc(vec_done, 1)
                    after_end = steps.inc()
                if norming:
                    dve.wait_ge(std_ready, a)
                    nc.vector.reciprocal(rstd[:, both(a - 2)], std[:, 0:2]).then_inc(vec_done, 1)
                    after_rstd = steps.inc()
                if scanning:
                    scan(g, b, 1)
                if attending:
                    after_add = add_packed(0, a)
                if packing:
                    dve.wait_ge(vec_done, after_end)
                    for s in range(2):
                        nc.vector.tensor_scalar(below[:, s, :], iota_q[:, :], keys[:, s, SLOTS:SLOTS + 1], None,
                                                ALU.is_lt).then_inc(vec_done, 1)
                        after_below = steps.inc()
                if norming:
                    dve.wait_ge(vec_done, after_rstd)
                    nc.vector.scalar_tensor_tensor(shift[:, both(a - 2)], mean_var[:, :, 0], -1.0,
                                                   rstd[:, both(a - 2)], ALU.mult, ALU.mult).then_inc(ln_ready, 1)
                if scanning:
                    scan(g, b, 2)
                if attending:
                    after_leaky = leaky(0, after_add)
                if packing:
                    dve.wait_ge(vec_done, after_below)
                    for s in range(2):
                        t = 2 * (g - 2) + s
                        done = nc.vector.scalar_tensor_tensor(
                            pick8[:, bass.ds(t, 1), 0, :], iota_q[:, :].unsqueeze(1), end_all[:, bass.ds(t, 1)],
                            below[:, s:s + 1, :], ALU.is_lt, ALU.subtract)
                    done.then_inc(pick_ready, 1)
                if scanning:
                    scan(g, b, 3)
                if attending:
                    after_mask = mask(0, a, after_leaky)
                if listing:
                    dve.wait_ge(adj_scanned, 2 * QUARTERS * g)
                    nc.vector.tensor_tensor(key[:, :, :], chunk_base[:, :, :, :].rearrange("p s c k -> p s (c k)"),
                                            f, ALU.subtract).then_inc(vec_done, 1)
                    after_key = steps.inc()
                if scanning:
                    scan(g, b, 4)
                if attending:
                    after_max = row_max(0, after_mask)
                if listing:
                    dve.wait_ge(vec_done, after_key)
                    nc.vector.scalar_tensor_tensor(cand[:, :, :], f, float(CH), key[:, :, :], ALU.is_lt, ALU.mult)\
                        .then_inc(vec_done, 1)
                    after_cand = steps.inc()
                if scanning:
                    scan(g, b, 5)
                if attending:
                    minus_max(0, after_max)
                if listing:
                    dve.wait_ge(vec_done, after_cand)
                    nc.vector.tensor_tensor(is_self[:, :, :], cand[:, :, :],
                                            self_key[:, both(g - 1)].unsqueeze(2)
                                            .to_broadcast([P, 2, CHUNKS * FOUND]), ALU.is_equal).then_inc(vec_done, 1)
                    after_self = steps.inc()
                    nc.vector.tensor_tensor(last_found[:, :, :], last_found[:, :, :],
                                            found[:, p, :, :, FOUND - 1], ALU.min).then_inc(vec_done, 1)
                    steps.inc()
                if scanning:
                    scan(g, b, 6)
                if packing:
                    dve.wait_ge(info_in_psum, g - 1)
                    nc.vector.tensor_copy(info[:, :, :], ps_info).then_inc(vec_done, 1)
                    after_info = steps.inc()
                if listing:
                    dve.wait_ge(vec_done, after_self)
                    nc.vector.tensor_reduce(self_flag[:, both(g - 1)], is_self[:, :, :], AX, ALU.max)\
                        .then_inc(vec_done, 1)
                    after_flag = steps.inc()
                    nc.vector.scalar_tensor_tensor(cand[:, :, :], is_self[:, :, :], 0.0, cand[:, :, :],
                                                   ALU.is_equal, ALU.mult).then_inc(vec_done, 1)
                    after_others = steps.inc()
                if scanning:
                    scan(g, b, 7)
                if attending:
                    after_total = row_total(0, a)
                if packing:
                    dve.wait_ge(vec_done, after_info)
                    nc.vector.tensor_scalar(rank[:, :], info[:, :, PACKED], -1.0, col_q[:, 0:1], ALU.mult, ALU.add)\
                        .then_inc(vec_done, 1)
                    after_rank = steps.inc()
                if listing:
                    dve.wait_ge(vec_done, after_others)
                    nc.vector.tensor_reduce(cand_sum[:, both(g - 1)], cand[:, :, :], AX, ALU.add)
                    for s in range(2):
                        done = nc.vector.max(keys[:, s, 0:FOUND], cand[:, s, :])
                    done.then_inc(vec_done, 1)
                    after_first = steps.inc()
                if scanning:
                    scan(g, b, 8)
                if attending:
                    after_inv = invert(0, after_total)
                if packing:
                    dve.wait_ge(vec_done, after_rank)
                    nc.vector.tensor_tensor(place[:, both(g - 2), :],
                                            iota_q[:, 0:PACKED].unsqueeze(1).to_broadcast([P, 2, PACKED]),
                                            rank[:, :].unsqueeze(2).to_broadcast([P, 2, PACKED]), ALU.is_equal)\
                        .then_inc(vec_done, 1)
                    after_place = steps.inc()
                if listing:
                    dve.wait_ge(vec_done, after_first)
                    dve.sem_inc(dve_passed, 1)
                    for s in range(2):
                        done = nc.vector.match_replace(out=key[:, s, :], in_to_replace=keys[:, s, 0:FOUND],
                                                       in_values=cand[:, s, :], imm_value=0.0)
                    done.then_inc(vec_done, 1)
                    after_rest = steps.inc()
                if scanning:
                    scan(g, b, 9)
                if attending:
                    normalise(0, a, after_inv, steady or a >= 1)
                if packing:
                    dve.wait_ge(vec_done, after_place)
                    nc.vector.tensor_tensor(own_key[:, :, :], info[:, :, 0:PACKED], place[:, both(g - 2), :],
                                            ALU.mult).then_inc(vec_done, 1)
                    after_own_key = steps.inc()
                    for s in range(2):
                        done = nc.vector.tensor_scalar(pick8[:, bass.ds(2 * (g - 2) + s, 1), 1, :],
                                                       iota_o[:, :].unsqueeze(1), info[:, s, PACKED + 1:PACKED + 2],
                                                       None, ALU.is_equal)
                    done.then_inc(places_ready, 1)
                if listing:
                    dve.wait_ge(vec_done, after_rest)
                    dve.sem_inc(dve_passed, 1)
                    for s in range(2):
                        done = nc.vector.max(keys[:, s, FOUND:SLOTS], key[:, s, :])
                    done.then_inc(keys_ready, 1)
                if scanning:
                    scan(g, b, 10)
                if listing:
                    dve.wait_ge(keys_ready, g)
                    nc.vector.tensor_scalar(has_packed[:, :, :], keys[:, :, DIRECT:SLOTS], 0.0, None, ALU.is_gt)\
                        .then_inc(vec_done, 1)
                    after_has = steps.inc()
                if packing:
                    dve.wait_ge(vec_done, after_own_key)
                    nc.vector.tensor_reduce(packed_key[:, :], own_key[:, :, :], AX, ALU.add).then_inc(vec_done, 1)
                    after_packed_key = steps.inc()
                if scanning:
                    scan(g, b, 11)
                if attending:
                    after_placed = place_probs(0, a)
                if listing:
                    dve.wait_ge(vec_done, after_has)
                    nc.vector.tensor_reduce(count[:, :], has_packed[:, :, :], AX, ALU.add).then_inc(counts_ready, 1)
                if packing:
                    dve.wait_ge(vec_done, after_packed_key)
                    nc.vector.tensor_scalar(idx_all[:, both(g - 2), DIRECT], packed_key[:, :], -1.0, float(N),
                                            ALU.mult, ALU.add).then_inc(vec_done, 1)
                    after_idx = steps.inc()
                if scanning:
                    scan(g, b, 12)
                if attending:
                    packed_weights(0, a, after_placed)
                if adding:
                    residual(0, a - 1, p)
                if listing:
                    nc.vector.tensor_scalar(idx_all[:, both(g - 1), 0:DIRECT], keys[:, :, 0:DIRECT], -1.0, float(N),
                                            ALU.mult, ALU.add)
                    nc.vector.tensor_scalar(pen[:, both(g - 1), 0:SLOTS], keys[:, :, 0:SLOTS], 0.0, MASKED,
                                            ALU.is_equal, ALU.mult)
                if scanning:
                    scan(g, b, 13)
                if adding:
                    dve.wait_ge(x1_ready, a)
                    dve.sem_inc(dve_passed, 1)
                    for s in range(2):
                        done = nc.vector.bn_stats(stats[:, s, :], x_sb[:, bass.ds(2 * (a - 1) + s, 1), :])
                    done.then_inc(vec_done, 1)
                    after_stats = steps.inc()
                if listing:
                    dve.wait_ge(vec_done, after_flag)
                    nc.vector.tensor_scalar(pen[:, both(g - 1), SLOTS], self_flag[:, both(g - 1)], 0.0, MASKED,
                                            ALU.is_equal, ALU.mult)
                    nc.vector.tensor_reduce(keys_sum[:, both(g - 1)], keys[:, :, 0:SLOTS], AX, ALU.add)\
                        .then_inc(vec_done, 1)
                    steps.inc()
                if scanning:
                    scan(g, b, 14)
                if adding:
                    dve.wait_ge(vec_done, after_stats)
                    if norming:
                        dve.wait_ge(ln_ready, a)
                    dve.sem_inc(dve_passed, 1)
                    for s in range(2):
                        done = nc.vector.bn_aggr(mean_var[:, s, :], stats[:, s, :])
                    done.then_inc(var_ready, 1)
                if packing:
                    dve.wait_ge(vec_done, after_idx)
                    dve.sem_inc(dve_passed, 1)
                    give_indices(0, g - 2, b)
                if scanning:
                    scan(g, b, 15)

            dve.wait_ge(consts_ready, N_CONSTS)
            for g in range(LAG + 2):
                stream_step(g, g % 2, False)
            before = steps.n
            with dve.Fori((LAG + 2) // 2, NG // 2) as d:
                STEPS = 29
                steps.base = before + (2 * d - (LAG + 2)) * STEPS
                steps.n = 0
                for b in range(2):
                    stream_step(2 * d + b, b, True)
                assert steps.n == 2 * STEPS, steps.n
            steps.base, steps.n = 0, before + (NG - LAG - 2) * STEPS
            for g in range(NG, NG + LAG + 2):
                stream_step(g, g % 2, False)

            dve.wait_ge(vec_done, steps.now())
            nc.vector.tensor_reduce(row_flag[:, 0:1], last_found[:, :, :].rearrange("p s c -> p (s c)"), AX, ALU.min)
            nc.vector.tensor_scalar(flags[:, 3, :], end_all[:, :], float(P), None, ALU.is_gt)
            nc.vector.tensor_tensor(flags[:, 0, :], cand_sum[:, :], keys_sum[:, :], ALU.not_equal)
            nc.vector.tensor_tensor(flags[:, 1, :], pen[:, :, 0], pen[:, :, SLOTS], ALU.add).then_inc(vec_done, 1)
            dve.wait_ge(vec_done, steps.inc())
            nc.vector.tensor_scalar(row_flag[:, 2:3], row_flag[:, 0:1], float(CH), None, ALU.is_lt)
            nc.vector.tensor_reduce(row_flag[:, 1:2], flags[:, 0, :], AX, ALU.max)
            nc.vector.tensor_reduce(row_flag[:, 4:5], flags[:, 3, :], AX, ALU.max)
            nc.vector.tensor_scalar(flags[:, 2, :], flags[:, 1, :], 1.5 * MASKED, None, ALU.is_lt)\
                .then_inc(vec_done, 1)
            dve.wait_ge(vec_done, steps.inc())
            nc.vector.tensor_reduce(row_flag[:, 3:4], flags[:, 2, :], AX, ALU.max).then_inc(vec_done, 1)
            dve.wait_ge(vec_done, steps.inc())
            nc.vector.tensor_reduce(any_flag[:, :], row_flag[:, 1:5], AX, ALU.max).then_inc(flag_in, 1)
            dve.wait_ge(flag_summed, 1)
            nc.vector.tensor_copy(dense_flag[0:1, 0:1], ps_flag).then_inc(flag_ready, 1)
            dve.wait_ge(flag_ready, 1)

            def list_step(a, b, first, last):
                put_back(1, a, b)
                add_direct(1, a, b)
                if not last:
                    give_indices(1, a + 2, b)
                if not first:
                    residual(1, a - 1, 1 - b)
                after = add_packed(1, a)
                after = leaky(1, after)
                after = mask(1, a, after)
                after = row_max(1, after)
                minus_max(1, after)
                after = row_total(1, a)
                after = invert(1, after)
                normalise(1, a, after, True)
                dve.wait_ge(probs_ready, NG + a + 1)
                dve.wait_ge(sums_ready, NG + a)
                for s in range(2):
                    rows = gath[:, b, s, 0:DIRECT, 0:D].rearrange("p k (h d) -> p k h d", h=HEADS[1])
                    w = prob[:, s, :, 0:DIRECT].rearrange("p h k -> p k h")
                    nc.vector.tensor_tensor(rows, rows, w.unsqueeze(3).to_broadcast([P, DIRECT, HEADS[1], HD]),
                                            ALU.mult)
                    rows = tab[:, bass.ds(2 * a + s, 1), 0:D].rearrange("p o (h d) -> p (o h) d", h=HEADS[1])
                    w = prob[:, s, :, SLOTS]
                    nc.vector.tensor_tensor(own[:, s, :].rearrange("p (h d) -> p h d", h=HEADS[1]), rows,
                                            w.unsqueeze(2).to_broadcast([P, HEADS[1], HD]), ALU.mult)\
                        .then_inc(weighted, 1)
                packed_weights(1, a, place_probs(1, a))
                dve.wait_ge(packed_w_ready, NG + a + 1)
                for s in range(2):
                    rows = gath[:, b, s, DIRECT, 0:D].rearrange("p (h d) -> p h d", h=HEADS[1])
                    nc.vector.tensor_tensor(rows, rows, packed_w[:, s, :].unsqueeze(2)
                                            .to_broadcast([P, HEADS[1], HD]), ALU.mult)\
                        .then_inc(packed_weighted, 1)

            dense = dve.value_load(dense_flag[0:1, 0:1])
            listed = steps.n
            with dve.If(dense > 0):
                for layer in range(2):
                    norm_all(1 + NG + layer + 1, 2 + layer)
                    dve.wait_ge(tab_ready, (2 + layer) * NG)
                    for n, (_, cols) in enumerate(PASSES):
                        if PASSES[n][0] != layer:
                            continue
                        head = cols.start // (D // HEADS[layer])
                        width = cols.stop - cols.start
                        with dve.Fori(0, NT) as t:
                            k = n * NT + t
                            nc.vector.tensor_scalar(h_sb[:, 0, :], ident[:, :],
                                                    tab[:, bass.ds(t, 1), F_DST + head:F_DST + head + 1]
                                                    .rearrange("p o c -> p (o c)"), None, ALU.mult)\
                                .then_inc(d_diag_ready, 1)
                            dve.wait_ge(d_spread, k + 1)
                            nc.vector.tensor_scalar(d_f_dst[:, bass.ds(P * t, P)], ps_h[:, 0, 0:P], 0.0, None, ALU.add)\
                                .then_inc(vec_done, 1)
                        steps.n += NT
                        dve.wait_ge(vec_done, steps.now())
                        before = steps.n
                        with dve.Fori(0, NT) as t:
                            tile = n * NT + t
                            steps.base, steps.n = before + t * DENSE_STEPS, 0
                            f_src = tab[:, bass.ds(t, 1), F_SRC + head:F_SRC + head + 1].rearrange("p o c -> p (o c)")
                            dve.wait_ge(d_adj_landed, 16 * (tile + 1))
                            nc.vector.tensor_scalar(d_pen, d_adj_int, 0.0, None, ALU.is_gt).then_inc(vec_done, 1)
                            dve.wait_ge(vec_done, steps.inc())
                            nc.vector.tensor_scalar(d_pen, d_pen, 1.0, BIG, ALU.subtract, ALU.mult)\
                                .then_inc(vec_done, 1)
                            steps.inc()
                            nc.vector.tensor_scalar(d_score, d_f_dst, f_src, None, ALU.add).then_inc(vec_done, 1)
                            dve.wait_ge(vec_done, steps.inc())
                            nc.vector.scalar_tensor_tensor(d_score, d_score, SLOPE, d_score, ALU.mult, ALU.max)\
                                .then_inc(vec_done, 1)
                            dve.wait_ge(vec_done, steps.inc())
                            nc.vector.tensor_tensor(d_score, d_score, d_pen, ALU.add).then_inc(vec_done, 1)
                            dve.wait_ge(vec_done, steps.inc())
                            nc.vector.tensor_reduce(d_top[:, :], d_score, AX, ALU.max).then_inc(vec_done, 1)
                            dve.wait_ge(vec_done, steps.inc())
                            nc.vector.tensor_scalar(d_top[:, :], d_top[:, :], -1.0, None, ALU.mult)\
                                .then_inc(d_scores_ready, 1)
                            dve.wait_ge(d_exps_ready, tile + 1)
                            nc.vector.scalar_tensor_tensor(d_score, d_pen, 0.0, d_score, ALU.is_equal, ALU.mult)\
                                .then_inc(d_probs_ready, 1)
                            dve.wait_ge(d_probs_ready, tile + 1)
                            nc.vector.tensor_reduce(d_total[:, :], d_score, AX, ALU.add).then_inc(vec_done, 1)
                            dve.wait_ge(vec_done, steps.inc())
                            nc.vector.reciprocal(d_total[:, :], d_total[:, :]).then_inc(vec_done, 1)
                            after_inv = steps.inc()
                            assert steps.n == DENSE_STEPS, steps.n
                            with dve.Fori(0, NT) as j:
                                nc.vector.tensor_copy(h_sb[:, 1, :], d_score[:, bass.ds(P * j, P)])\
                                    .then_inc(d_block_ready, 1)
                                dve.wait_ge(d_turned, tile * NT + j + 1)
                                nc.vector.tensor_copy(ht_sb[:, 0, :], ps_t[0][:, 0:P]).then_inc(d_turned_copied, 1)
                            dve.wait_ge(d_sum_ready, tile + 1)
                            dve.wait_ge(d_rest_landed, 16 * (tile + 1))
                            dve.wait_ge(vec_done, after_inv)
                            nc.vector.scalar_tensor_tensor(own[:, 0, 0:width], ps_sum[:, 0, 0:width], d_total[:, 0:1],
                                                           own[:, 1, 0:width], ALU.mult, ALU.add)\
                                .then_inc(d_out_ready, 1)
                        steps.base, steps.n = 0, before + NT * DENSE_STEPS
            with dve.Else():
                steps.n = listed
                give_indices(1, 0, 0)
                give_indices(1, 1, 1)
                L1_STEPS = 7
                before = steps.n
                list_step(0, 0, True, False)
                list_step(1, 1, False, False)
                assert steps.n == before + 2 * L1_STEPS, steps.n - before
                before = steps.n
                with dve.Fori(1, NG // 2 - 1) as d:
                    steps.base = before + (2 * d - 2) * L1_STEPS
                    steps.n = 0
                    for b in range(2):
                        list_step(2 * d + b, b, False, False)
                steps.base, steps.n = 0, before + (NG - 4) * L1_STEPS
                list_step(NG - 2, 0, False, True)
                list_step(NG - 1, 1, False, True)
                residual(1, NG - 1, 1)


def kernel(x, adj, L0_gnn_weight, L0_gnn_weight_a1, L0_gnn_weight_a2, L1_gnn_W, L1_gnn_a):
    import numpy as np
    import concourse.bacc as bacc
    from concourse.bass_utils import run_bass_kernel_spmd

    nc = bacc.Bacc("TRN2", target_bir_lowering=False, num_devices=1)
    arrays = {
        "x": np.ascontiguousarray(x), "adj": np.ascontiguousarray(adj),
        "w0": np.ascontiguousarray(L0_gnn_weight), "w0_a1": np.ascontiguousarray(L0_gnn_weight_a1),
        "w0_a2": np.ascontiguousarray(L0_gnn_weight_a2), "w1": np.ascontiguousarray(L1_gnn_W),
        "a1h": np.ascontiguousarray(L1_gnn_a).reshape(-1, 1),
    }
    args = [nc.dram_tensor(n, a.shape, mybir.dt.from_np(a.dtype), kind="ExternalInput").ap()
            for n, a in arrays.items()]
    out = nc.dram_tensor("out", arrays["x"].shape, F32, kind="ExternalOutput").ap()
    build(nc, *args, out)
    r = run_bass_kernel_spmd(nc, [arrays], core_ids=[0])
    return r.results[0]["out"]
```
